# Optimizing a Trainium2 kernel written in Bass

```python
import numpy as np
import jax
import jax.numpy as jnp

def _softmax(x, axis=-1):
    return jax.nn.softmax(x, axis=axis)

def _gelu(x):
    return jax.nn.gelu(x, approximate=True)

def _silu(x):
    return jax.nn.silu(x)

def _sigmoid(x):
    return jax.nn.sigmoid(x)

def _layernorm(x, axis=-1, eps=1e-05):
    m = jnp.mean(x, axis=axis, keepdims=True)
    v = jnp.var(x, axis=axis, keepdims=True)
    return (x - m) / jnp.sqrt(v + eps)

def _scatter_add(tgt, idx, src, axis=0):
    return tgt.at[idx].add(src)

def _segment_sum(src, seg, n):
    return jax.ops.segment_sum(src, seg, n)
kernel_name = 'mk_seq_preln_d1_jaxref_r4_409281'

def setup_inputs(seed: int=0):
    np.random.seed(seed)
    _w = jnp.asarray

    def _L0_attn_setup():
        import jax, jax.numpy as jnp
        from jax import lax
        import numpy as np
        B, S, D, H = (4, 512, 256, 16)
        HD = D // H
        EPS = 1e-08
        LN_EPS = 1e-05
        key = jax.random.key(seed)
        ks = jax.random.split(key, 8)
        sc = 1.0 / np.sqrt(D)
        return {'x': jax.random.normal(ks[0], (B, S, D), jnp.float32), 'time_mix_r': jnp.full((1, 1, D), 0.5, jnp.float32), 'time_mix_k': jnp.full((1, 1, D), 0.5, jnp.float32), 'time_mix_v': jnp.full((1, 1, D), 0.5, jnp.float32), 'W_r': jax.random.normal(ks[1], (D, D), jnp.float32) * sc, 'W_k': jax.random.normal(ks[2], (D, D), jnp.float32) * sc, 'W_v': jax.random.normal(ks[3], (D, D), jnp.float32) * sc, 'W_o': jax.random.normal(ks[4], (D, D), jnp.float32) * sc, 'time_decay': jax.random.normal(ks[5], (H, HD), jnp.float32) * 0.1 - 5.0, 'time_first': jax.random.normal(ks[6], (H, HD), jnp.float32) * 0.1, 'ln_gamma': jnp.ones((D,), jnp.float32), 'ln_beta': jnp.zeros((D,), jnp.float32)}
    _L0_attn_in = _L0_attn_setup()

    def _L0_ffn_setup():
        import jax, jax.numpy as jnp
        import numpy as np
        DIM = 256
        DEPTH = 2
        HEADS = 8
        DIM_HEAD = 64
        WINDOW = 128
        INNER = HEADS * DIM_HEAD
        HID = int(DIM * 4 * 2 / 3)
        B, N = (2, 2048)
        QK_SCALE = 8.0

        def shift_token(t):
            t1, t2 = jnp.split(t, 2, axis=-1)
            t2 = jnp.pad(t2, ((0, 0), (1, 0), (0, 0)))[:, :-1]
            return jnp.concatenate([t1, t2], axis=-1)

        def l2norm(t):
            return t / jnp.clip(jnp.linalg.norm(t, axis=-1, keepdims=True), 1e-12)

        def rotate_half(x):
            x1, x2 = jnp.split(x, 2, axis=-1)
            return jnp.concatenate([-x2, x1], axis=-1)

        def rotary_xpos(q, k):
            n = q.shape[-2]
            half_idx = jnp.arange(0, DIM_HEAD, 2, dtype=jnp.float32)
            inv_freq = 1.0 / 10000.0 ** (half_idx / DIM_HEAD)
            t = jnp.arange(n, dtype=jnp.float32)
            freqs = t[:, None] * inv_freq[None, :]
            freqs = jnp.concatenate([freqs, freqs], axis=-1)
            base = (half_idx + 0.4 * DIM_HEAD) / (1.4 * DIM_HEAD)
            power = (t - n // 2) / float(WINDOW // 2)
            scale = base[None, :] ** power[:, None]
            scale = jnp.concatenate([scale, scale], axis=-1)
            cos, sin = (jnp.cos(freqs), jnp.sin(freqs))
            q = q * cos * scale + rotate_half(q) * sin * scale
            k = k * cos / scale + rotate_half(k) * sin / scale
            return (q, k)

        def local_attention(q, k, v):
            b, h, n, d = q.shape
            w = n // WINDOW
            bq = q.reshape(b, h, w, WINDOW, d) * QK_SCALE
            bk = k.reshape(b, h, w, WINDOW, d)
            bv = v.reshape(b, h, w, WINDOW, d)

            def look_around(t):
                p = jnp.pad(t, ((0, 0), (0, 0), (1, 0), (0, 0), (0, 0)))
                return jnp.concatenate([p[:, :, :w], p[:, :, 1:]], axis=3)
            bk, bv = (look_around(bk), look_around(bv))
            bt = jnp.arange(n).reshape(w, WINDOW)
            btp = jnp.pad(bt, ((1, 0), (0, 0)), constant_values=-1)
            btk = jnp.concatenate([btp[:w], btp[1:]], axis=1)
            sim = jnp.einsum('bhwid,bhwjd->bhwij', bq, bk)
            i = bt[:, :, None]
            j = btk[:, None, :]
            mask = (i < j) | (i > j + WINDOW) | (j == -1)
            sim = jnp.where(mask, -jnp.finfo(sim.dtype).max, sim)
            attn = jax.nn.softmax(sim, axis=-1)
            out = jnp.einsum('bhwij,bhwjd->bhwid', attn, bv)
            return out.reshape(b, h, n, d)

        def _layer(x, wqkv, qs, ksc, wo, lg, lb, w1, b1, w2, b2):
            b, n, _ = x.shape
            h = shift_token(x)
            qkv = h @ wqkv
            q, k, v = jnp.split(qkv, 3, axis=-1)
            to_heads = lambda t: t.reshape(b, n, HEADS, DIM_HEAD).transpose(0, 2, 1, 3)
            q, k, v = (to_heads(q), to_heads(k), to_heads(v))
            q = l2norm(q) * qs
            k = l2norm(k) * ksc
            q, k = rotary_xpos(q, k)
            o = local_attention(q, k, v)
            o = o.transpose(0, 2, 1, 3).reshape(b, n, INNER)
            x = x + o @ wo
            h = shift_token(x)
            mu = h.mean(-1, keepdims=True)
            var = h.var(-1, keepdims=True)
            h = (h - mu) / jnp.sqrt(var + 1e-05) * lg + lb
            h = h @ w1 + b1
            a, g = jnp.split(h, 2, axis=-1)
            h = a * jax.nn.gelu(g, approximate=False)
            x = x + h @ w2 + b2
            return x
        key = jax.random.key(seed)
        ks = jax.random.split(key, 6)
        return {'x': jax.random.normal(ks[0], (B, N, DIM), jnp.float32), 'wqkv': jax.random.normal(ks[1], (DEPTH, DIM, 3 * INNER), jnp.float32) * 0.02, 'q_scale': jnp.ones((DEPTH, DIM_HEAD), jnp.float32), 'k_scale': jnp.ones((DEPTH, DIM_HEAD), jnp.float32), 'wo': jax.random.normal(ks[2], (DEPTH, INNER, DIM), jnp.float32) * 0.02, 'ln_g': jnp.ones((DEPTH, DIM), jnp.float32), 'ln_b': jnp.zeros((DEPTH, DIM), jnp.float32), 'w1': jax.random.normal(ks[3], (DEPTH, DIM, 2 * HID), jnp.float32) * 0.02, 'b1': jnp.zeros((DEPTH, 2 * HID), jnp.float32), 'w2': jax.random.normal(ks[4], (DEPTH, HID, DIM), jnp.float32) * 0.02, 'b2': jnp.zeros((DEPTH, DIM), jnp.float32)}
    _L0_ffn_in = _L0_ffn_setup()
    _d = {'L0_attn_x': _L0_attn_in['x'], 'L0_attn_time_mix_r': _L0_attn_in['time_mix_r'], 'L0_attn_time_mix_k': _L0_attn_in['time_mix_k'], 'L0_attn_time_mix_v': _L0_attn_in['time_mix_v'], 'L0_attn_W_r': _L0_attn_in['W_r'], 'L0_attn_W_k': _L0_attn_in['W_k'], 'L0_attn_W_v': _L0_attn_in['W_v'], 'L0_attn_W_o': _L0_attn_in['W_o'], 'L0_attn_time_decay': _L0_attn_in['time_decay'], 'L0_attn_time_first': _L0_attn_in['time_first'], 'L0_attn_ln_gamma': _L0_attn_in['ln_gamma'], 'L0_attn_ln_beta': _L0_attn_in['ln_beta'], 'L0_ffn_wqkv': _L0_ffn_in['wqkv'], 'L0_ffn_q_scale': _L0_ffn_in['q_scale'], 'L0_ffn_k_scale': _L0_ffn_in['k_scale'], 'L0_ffn_wo': _L0_ffn_in['wo'], 'L0_ffn_ln_g': _L0_ffn_in['ln_g'], 'L0_ffn_ln_b': _L0_ffn_in['ln_b'], 'L0_ffn_w1': _L0_ffn_in['w1'], 'L0_ffn_b1': _L0_ffn_in['b1'], 'L0_ffn_w2': _L0_ffn_in['w2'], 'L0_ffn_b2': _L0_ffn_in['b2']}
    _x0 = _d['L0_attn_x']
    _d['L0_attn_x'] = jax.random.normal(jax.random.fold_in(jax.random.key(seed), 1), (2, 4096, 256), dtype=_x0.dtype)
    del _x0
    return _d

def reference(L0_attn_x, L0_attn_time_mix_r, L0_attn_time_mix_k, L0_attn_time_mix_v, L0_attn_W_r, L0_attn_W_k, L0_attn_W_v, L0_attn_W_o, L0_attn_time_decay, L0_attn_time_first, L0_attn_ln_gamma, L0_attn_ln_beta, L0_ffn_wqkv, L0_ffn_q_scale, L0_ffn_k_scale, L0_ffn_wo, L0_ffn_ln_g, L0_ffn_ln_b, L0_ffn_w1, L0_ffn_b1, L0_ffn_w2, L0_ffn_b2):

    def _L0_attn_ref(x, time_mix_r, time_mix_k, time_mix_v, W_r, W_k, W_v, W_o, time_decay, time_first, ln_gamma, ln_beta):
        import jax, jax.numpy as jnp
        from jax import lax
        import numpy as np
        B, S, D, H = (4, 512, 256, 16)
        HD = D // H
        EPS = 1e-08
        LN_EPS = 1e-05
        b, s, d = x.shape
        h, hd = time_decay.shape
        shifted = jnp.pad(x[:, :-1, :], ((0, 0), (1, 0), (0, 0)))
        xr = x * time_mix_r + shifted * (1.0 - time_mix_r)
        xk = x * time_mix_k + shifted * (1.0 - time_mix_k)
        xv = x * time_mix_v + shifted * (1.0 - time_mix_v)
        r = (xr @ W_r.T).reshape(b, s, h, hd)
        k = (xk @ W_k.T).reshape(b, s, h, hd)
        v = (xv @ W_v.T).reshape(b, s, h, hd)
        w = -jnp.exp(time_decay)
        u = time_first

        def step(carry, kv):
            a, bst = carry
            kt, vt = kv
            wk = kt + u
            p = jnp.maximum(bst, wk)
            e1 = jnp.exp(bst - p)
            e2 = jnp.exp(wk - p)
            out = (e1 * a + e2 * vt) / (e1 + e2 + EPS)
            ww = bst + w
            p2 = jnp.maximum(ww, kt)
            e1b = jnp.exp(ww - p2)
            e2b = jnp.exp(kt - p2)
            a_new = e1b * a + e2b * vt
            b_new = p2 + jnp.log(e1b + e2b + EPS)
            return ((a_new, b_new), out)
        a0 = jnp.zeros((b, h, hd), x.dtype)
        b0 = jnp.full((b, h, hd), -1e+38, x.dtype)
        kT = jnp.moveaxis(k, 1, 0)
        vT = jnp.moveaxis(v, 1, 0)
        _, outs = lax.scan(step, (a0, b0), (kT, vT))
        wkv = jnp.moveaxis(outs, 0, 1)
        rwkv = jax.nn.sigmoid(r) * wkv
        mean = jnp.mean(rwkv, axis=(1, 3), keepdims=True)
        var = jnp.var(rwkv, axis=(1, 3), keepdims=True)
        normed = (rwkv - mean) * lax.rsqrt(var + LN_EPS)
        normed = normed * ln_gamma.reshape(1, 1, h, hd) + ln_beta.reshape(1, 1, h, hd)
        return normed.reshape(b, s, d) @ W_o.T

    def _L0_ffn_ref(x, wqkv, q_scale, k_scale, wo, ln_g, ln_b, w1, b1, w2, b2):
        import jax, jax.numpy as jnp
        import numpy as np
        DIM = 256
        DEPTH = 2
        HEADS = 8
        DIM_HEAD = 64
        WINDOW = 128
        INNER = HEADS * DIM_HEAD
        HID = int(DIM * 4 * 2 / 3)
        B, N = (2, 2048)
        QK_SCALE = 8.0

        def shift_token(t):
            t1, t2 = jnp.split(t, 2, axis=-1)
            t2 = jnp.pad(t2, ((0, 0), (1, 0), (0, 0)))[:, :-1]
            return jnp.concatenate([t1, t2], axis=-1)

        def l2norm(t):
            return t / jnp.clip(jnp.linalg.norm(t, axis=-1, keepdims=True), 1e-12)

        def rotate_half(x):
            x1, x2 = jnp.split(x, 2, axis=-1)
            return jnp.concatenate([-x2, x1], axis=-1)

        def rotary_xpos(q, k):
            n = q.shape[-2]
            half_idx = jnp.arange(0, DIM_HEAD, 2, dtype=jnp.float32)
            inv_freq = 1.0 / 10000.0 ** (half_idx / DIM_HEAD)
            t = jnp.arange(n, dtype=jnp.float32)
            freqs = t[:, None] * inv_freq[None, :]
            freqs = jnp.concatenate([freqs, freqs], axis=-1)
            base = (half_idx + 0.4 * DIM_HEAD) / (1.4 * DIM_HEAD)
            power = (t - n // 2) / float(WINDOW // 2)
            scale = base[None, :] ** power[:, None]
            scale = jnp.concatenate([scale, scale], axis=-1)
            cos, sin = (jnp.cos(freqs), jnp.sin(freqs))
            q = q * cos * scale + rotate_half(q) * sin * scale
            k = k * cos / scale + rotate_half(k) * sin / scale
            return (q, k)

        def local_attention(q, k, v):
            b, h, n, d = q.shape
            w = n // WINDOW
            bq = q.reshape(b, h, w, WINDOW, d) * QK_SCALE
            bk = k.reshape(b, h, w, WINDOW, d)
            bv = v.reshape(b, h, w, WINDOW, d)

            def look_around(t):
                p = jnp.pad(t, ((0, 0), (0, 0), (1, 0), (0, 0), (0, 0)))
                return jnp.concatenate([p[:, :, :w], p[:, :, 1:]], axis=3)
            bk, bv = (look_around(bk), look_around(bv))
            bt = jnp.arange(n).reshape(w, WINDOW)
            btp = jnp.pad(bt, ((1, 0), (0, 0)), constant_values=-1)
            btk = jnp.concatenate([btp[:w], btp[1:]], axis=1)
            sim = jnp.einsum('bhwid,bhwjd->bhwij', bq, bk)
            i = bt[:, :, None]
            j = btk[:, None, :]
            mask = (i < j) | (i > j + WINDOW) | (j == -1)
            sim = jnp.where(mask, -jnp.finfo(sim.dtype).max, sim)
            attn = jax.nn.softmax(sim, axis=-1)
            out = jnp.einsum('bhwij,bhwjd->bhwid', attn, bv)
            return out.reshape(b, h, n, d)

        def _layer(x, wqkv, qs, ksc, wo, lg, lb, w1, b1, w2, b2):
            b, n, _ = x.shape
            h = shift_token(x)
            qkv = h @ wqkv
            q, k, v = jnp.split(qkv, 3, axis=-1)
            to_heads = lambda t: t.reshape(b, n, HEADS, DIM_HEAD).transpose(0, 2, 1, 3)
            q, k, v = (to_heads(q), to_heads(k), to_heads(v))
            q = l2norm(q) * qs
            k = l2norm(k) * ksc
            q, k = rotary_xpos(q, k)
            o = local_attention(q, k, v)
            o = o.transpose(0, 2, 1, 3).reshape(b, n, INNER)
            x = x + o @ wo
            h = shift_token(x)
            mu = h.mean(-1, keepdims=True)
            var = h.var(-1, keepdims=True)
            h = (h - mu) / jnp.sqrt(var + 1e-05) * lg + lb
            h = h @ w1 + b1
            a, g = jnp.split(h, 2, axis=-1)
            h = a * jax.nn.gelu(g, approximate=False)
            x = x + h @ w2 + b2
            return x
        for l in range(DEPTH):
            x = _layer(x, wqkv[l], q_scale[l], k_scale[l], wo[l], ln_g[l], ln_b[l], w1[l], b1[l], w2[l], b2[l])
        return x
    x = L0_attn_x
    x = x + _L0_attn_ref(_layernorm(x, axis=-1), L0_attn_time_mix_r, L0_attn_time_mix_k, L0_attn_time_mix_v, L0_attn_W_r, L0_attn_W_k, L0_attn_W_v, L0_attn_W_o, L0_attn_time_decay, L0_attn_time_first, L0_attn_ln_gamma, L0_attn_ln_beta)
    x = x + _L0_ffn_ref(_layernorm(x, axis=-1), L0_ffn_wqkv, L0_ffn_q_scale, L0_ffn_k_scale, L0_ffn_wo, L0_ffn_ln_g, L0_ffn_ln_b, L0_ffn_w1, L0_ffn_b1, L0_ffn_w2, L0_ffn_b2)
    return x

_drawn_inputs = setup_inputs


def setup_inputs(seed=0):
    import zlib

    import numpy as np

    out = dict(_drawn_inputs(seed))
    spreads = {'L0_attn_time_mix_r': (0.5, 0.2),
     'L0_attn_time_mix_k': (0.5, 0.2),
     'L0_attn_time_mix_v': (0.5, 0.2),
     'L0_attn_ln_gamma': (1.0, 0.2),
     'L0_attn_ln_beta': (0.0, 0.1),
     'L0_ffn_q_scale': (1.0, 0.6),
     'L0_ffn_k_scale': (1.0, 0.6),
     'L0_ffn_ln_g': (1.0, 0.6),
     'L0_ffn_ln_b': (0.0, 0.8),
     'L0_ffn_b1': (0.0, 0.8),
     'L0_ffn_b2': (0.0, 0.1)}
    factors = {'L0_attn_time_first': 36.641, 'L0_ffn_w1': 2.775, 'L0_ffn_w2': 2.751}
    for name, (base, spread) in spreads.items():
        noise = np.random.default_rng([zlib.crc32(name.encode()), seed]).standard_normal(out[name].shape)
        drawn = base * np.exp(spread * noise) if base else spread * noise
        out[name] = jnp.asarray(drawn.astype(out[name].dtype))
    for name, factor in factors.items():
        out[name] = (out[name] * factor).astype(out[name].dtype)
    return out
```

```python
from contextlib import ExitStack

import numpy as np
import concourse.bass as bass
from concourse import mybir

F32 = mybir.dt.float32
ALU = mybir.AluOpType
ACT = mybir.ActivationFunctionType
AX_X = mybir.AxisListType.X

NB = 2
T = 4096
NWIN = T // 128
NG = NB * NWIN
C = 256
CH = 512
NCH = T // CH
HID = 682
TAIL = HID - 5 * 128
LAG = 2
LOW = -1.0e38
MASKED = -1.0e30
EPS_W = 1e-8
EPS_LN = 1e-5

VEC = {"mix_r": 0, "mix_k": 2, "mix_v": 4, "decay": 6, "first": 8, "gamma": 10, "beta": 12,
       "lg": 14, "lb": 18, "b1a": 22, "b1g": 34}
NVEC = 46


class Queues:

    def __init__(self, nc, ctx):
        self.nc, self.ctx = nc, ctx
        self.sems, self.count = {}, {}
        self.q = {"pe": [], "act": [], "dve": [], "pool": [], "sp": []}

    def op(self, eng, fn, waits=(), sig=None, by=1):
        mark = None
        if sig is not None:
            if sig not in self.sems:
                self.sems[sig] = self.ctx.enter_context(self.nc.semaphore(sig))
                self.count[sig] = 0
            self.count[sig] += by
            mark = (sig, self.count[sig])
        self.q[eng].append((fn, [w for w in waits if w is not None], sig, by))
        return mark

    def run(self, eng, e):
        seen = {}
        for fn, waits, sig, by in self.q[eng]:
            for s, v in waits:
                if seen.get(s, 0) < v:
                    e.wait_ge(self.sems[s], v)
                    seen[s] = v
            if fn is None:
                continue
            ins = fn(e)
            if sig is not None:
                ins.then_inc(self.sems[sig], by)


def build(nc, x, wrkvo, wqkv, wo, w1, w2, b2, vec, qsk, tab, ident_d, shift_d, grp_d, mask_d, out):
    ctx = ExitStack()
    with ctx:
        Q = Queues(nc, ctx)
        op = Q.op
        rwkv_d = nc.dram_tensor("rwkv_scratch", (NB, 2, 128, T), F32, kind="Internal").ap()

        def sb(name, shape, c=ctx):
            return c.enter_context(nc.sbuf_tensor(name, [128] + shape, F32))

        PS = ctx.enter_context(nc.psum_tensor("ps", [128, 8, 512], F32))

        ident = sb("ident", [128])
        grp = sb("grp", [128])
        vecs = sb("vecs", [NVEC])
        Wr = sb("Wr", [4, 2, 256])
        WQ = sb("WQ", [2, 2, 1536])
        WO = sb("WO", [2, 4, 256])
        W1 = sb("W1", [2, 2, 1386])
        W2 = sb("W2", [2, 6, 256])
        wdec = sb("wdec", [2])
        wu = sb("wu", [2])
        epsw = sb("epsw", [1])
        mhalf = sb("mhalf", [16])
        bst = sb("bst", [NB, 2, NCH, 6])
        gsc = sb("gsc", [NB, 2])
        gsh = sb("gsh", [NB, 2])

        def V(name, i):
            return vecs[:, VEC[name] + i:VEC[name] + i + 1]

        def dma(dst, src, waits, sig):
            return op("sp", lambda e: e.dma_start(dst, src), waits, sig, 16)

        dma(ident[:, :], ident_d, [], "ld0")
        dma(vecs[:, :], vec, [], "ld0")
        dma(grp[:, :], grp_d, [], "ld0")
        LD0 = dma(Wr[:, :, :, :].rearrange("p m k n -> p (m k) n"),
                  wrkvo.rearrange("m (k p) n -> p (m k) n", p=128), [], "ld0")

        W1Z = op("pool", lambda e: e.memset(W1[:, :, :, 1280:1386], 0.0), [], "w1z")

        def load_ffn_weights():
            d = []
            for l in range(2):
                d.append((WQ[:, l, :, :], wqkv[l].rearrange("(k p) n -> p k n", p=128)))
                d.append((WO[:, l, :, :], wo[l].rearrange("(k p) n -> p k n", p=128)))
                w = w1[l].rearrange("(k p) n -> p k n", p=128)
                d.append((W1[:, l, :, 0:640], w[:, :, 0:640]))
                d.append((W1[:, l, :, 640:1280], w[:, :, HID:HID + 640]))
                d.append((W1[:, l, :, 1280:1280 + TAIL], w[:, :, 640:HID]))
                d.append((W1[:, l, :, 1344:1344 + TAIL], w[:, :, HID + 640:2 * HID]))
                d.append((W2[:, l, 0:5, :], w2[l, 0:640, :].rearrange("(k p) n -> p k n", p=128)))
                d.append((W2[0:TAIL, l, 5, :], w2[l, 640:HID, :]))
                d.append((W2[TAIL:TAIL + 1, l, 5, :], b2[l:l + 1, :]))
            m = None
            for dst, src in d:
                m = dma(dst, src, [W1Z], "ld1")
            return m

        MH = op("pool", lambda e: e.memset(mhalf[:, :], -0.5), [], "w1z")

        def inv_sqrt(ap, src, sig):
            w = ap.shape[-1]
            return op("pool", lambda e: e.tensor_tensor(ap, ap, mhalf[:, 0:w], ALU.pow), [src, MH], sig)

        EPSM = op("dve", lambda e: e.memset(epsw[:, :], EPS_W), [], "cst")
        m = op("act", lambda e: e.activation(wdec[:, :], vecs[:, VEC["decay"]:VEC["decay"] + 2], ACT.Exp),
               [LD0], "wdec_e")
        m = op("dve", lambda e: e.tensor_scalar(wdec[:, :], wdec[:, :], -1.0, None, ALU.mult), [m, LD0], "wdec")
        WU = op("dve", lambda e: e.tensor_tensor(wu[:, :], wdec[:, :], vecs[:, VEC["first"]:VEC["first"] + 2],
                                                 ALU.add), [m], "wdec")

        with ExitStack() as c1:
            xc = sb("xc", [2, 4, 256], c1)
            mvs = sb("mvs", [4, 8], c1)
            mva = sb("mva", [4, 2], c1)
            rsd = sb("rsd", [4], c1)
            xT = sb("xT", [NB, 2, CH + 1], c1)
            dx = sb("dx", [2, CH], c1)
            xm = sb("xm", [2, 2, CH], c1)
            kS = sb("kS", [3, 2, CH], c1)
            vS = sb("vS", [3, 2, CH], c1)
            sg = sb("sg", [3, 2, CH], c1)
            mS = sb("mS", [NB, 2, CH + 1], c1)
            bS = sb("bS", [NB, 2, CH + 1], c1)
            aS = sb("aS", [NB, 2, CH + 1], c1)
            Bc = sb("Bc", [NB, 2], c1)
            q1 = sb("q1", [2, CH], c1)
            km = sb("km", [2, CH], c1)
            BS = sb("BS", [2, CH], c1)
            q2 = sb("q2", [2, CH], c1)
            f = sb("f", [4, 2, CH], c1)
            n2 = sb("n2", [2, CH], c1)
            rw = sb("rw", [2, CH], c1)
            gmv = sb("gmv", [NB, 2, 2], c1)
            gtm = sb("gtm", [NB, 2, 4], c1)

            op("dve", lambda e: e.memset(xT[:, :, :, 0:1], 0.0), [], "cst")
            op("dve", lambda e: e.memset(mS[:, :, :, 0:1], LOW), [], "cst")
            op("dve", lambda e: e.memset(aS[:, :, :, 0:1], 0.0), [], "cst")
            op("dve", lambda e: e.memset(Bc[:, :, :], 0.0), [], "cst")
            CST = op("dve", lambda e: e.memset(bS[:, :, :, 0:1], LOW), [], "cst")

            M = {}

            def before(name, n, *rest):
                return M[(name, n, *rest)] if n >= 0 else None

            chunks = [(b, j) for j in range(NCH) for b in range(NB)]

            def load_x(n):
                b, j = chunks[n]
                p = n % 2
                M["ldx", n] = dma(xc[:, p, :, :], x[b, j * CH:(j + 1) * CH, :].rearrange("(w p) c -> p w c", p=128),
                                  [before("xtr", n - 2)], f"ldx{p}")

            def a_norm(n):
                p = n % 2
                for w in range(4):
                    s = op("dve", lambda e, w=w: e.bn_stats(mvs[:, w, 0:6], xc[:, p, w, :]), [M["ldx", n]], "a_st")
                    g = op("dve", lambda e, w=w: e.bn_aggr(mva[:, w, :], mvs[:, w, 0:6]), [s], "a_ag")
                r = op("dve", lambda e: e.tensor_scalar(rsd[:, :], mva[:, :, 1], EPS_LN, None, ALU.add),
                       [g], "a_rs")
                r = inv_sqrt(rsd[:, :], r, "a_rq")
                for w in range(4):
                    M["xn", n] = op("dve", lambda e, w=w: e.tensor_scalar(
                        xc[:, p, w, :], xc[:, p, w, :], mva[:, w, 0:1], rsd[:, w:w + 1], ALU.subtract, ALU.mult),
                        [r], "xn")

            def a_turn(n):
                b, j = chunks[n]
                p = n % 2
                for c in range(2):
                    for w in range(4):
                        M["xtr", n] = op("pe", lambda e, c=c, w=w: e.transpose(
                            PS[:, c, w * 128:(w + 1) * 128], xc[:, p, w, c * 128:(c + 1) * 128], ident[:, :]),
                            [M["xn", n], LD0, before("xT", n - 1)], "xtr" if (c, w) == (1, 3) else None)
                last = None
                if j:
                    last = op("act", lambda e: e.activation(xT[:, b, :, 0:1], xT[:, b, :, CH:CH + 1], ACT.Copy),
                              [M["mix", n - 2], M["xT", n - 2]], "xTc")
                M["xT", n] = op("act", lambda e: e.activation(xT[:, b, :, 1:CH + 1], PS[:, 0:2, :], ACT.Copy),
                                [M["xtr", n], last, CST], "xT")
                M["dx", n] = op("pool", lambda e: e.tensor_tensor(dx[:, :, :], xT[:, b, :, 1:CH + 1],
                                                                  xT[:, b, :, 0:CH], ALU.subtract),
                                [M["xT", n], before("rkv", n - 1, 2)], "dx")

            def mixed(i, c):
                return xm[:, i, c, :] if i < 2 else dx[:, c, :]

            def a_mix(n):
                b, j = chunks[n]
                for i, name in ((0, "mix_k"), (1, "mix_v"), (2, "mix_r")):
                    for c in range(2):
                        M["mix", n] = M["mix", n, i] = op("dve", lambda e, i=i, c=c, name=name: e.scalar_tensor_tensor(
                            out=mixed(i, c), in0=dx[:, c, :], scalar=V(name, c), in1=xT[:, b, c, 0:CH],
                            op0=ALU.mult, op1=ALU.add), [M["dx", n], before("rkv", n - 1, i)], "mix")

            def a_rkv(n):
                s = n % 3
                for i, wsel in ((0, 1), (1, 2), (2, 0)):
                    for g in range(2):
                        for c in range(2):
                            M["rkv", n, i] = op("pe", lambda e, i=i, g=g, c=c, wsel=wsel: e.matmul(
                                PS[:, 2 + 2 * i + g, :], Wr[:, wsel, c, g * 128:(g + 1) * 128], mixed(i, c),
                                start=(c == 0), stop=(c == 1)),
                                [M["mix", n, i], before("ev", n - 1, i)], f"rkv{i}" if (g, c) == (1, 1) else None)
                for i, dst, fn in ((0, kS, ACT.Copy), (1, vS, ACT.Copy), (2, sg, ACT.Sigmoid)):
                    M["ev", n, i] = op("act", lambda e, i=i, dst=dst, fn=fn: e.activation(
                        dst[:, s, :, :], PS[:, 2 + 2 * i:4 + 2 * i, :], fn),
                        [M["rkv", n, i], before("rw", n - 3)], f"ev{i}")

            def b_max(n):
                b, j = chunks[n]
                s = n % 3
                c = None
                if j:
                    c = op("dve", lambda e: e.tensor_copy(mS[:, b, :, 0:1], mS[:, b, :, CH:CH + 1]),
                           [M["msc", n - 2]], "msc0")
                for g in range(2):
                    M["msc", n] = op("dve", lambda e, g=g: e.tensor_tensor_scan(
                        mS[:, b, g, 1:CH + 1], wdec[:, g:g + 1].broadcast_to([128, CH]), kS[:, s, g, :],
                        mS[:, b, g, 0:1], ALU.add, ALU.max), [M["ev", n, 0], c, WU, CST, before("bS", n - 2)], "msc")
                for g in range(2):
                    M["q1", n] = op("dve", lambda e, g=g: e.scalar_tensor_tensor(
                        out=q1[:, g, :], in0=mS[:, b, g, 0:CH], scalar=wdec[:, g:g + 1], in1=mS[:, b, g, 1:CH + 1],
                        op0=ALU.add, op1=ALU.subtract), [M["msc", n]], "q1")
                M["km", n] = op("pool", lambda e: e.tensor_tensor(km[:, :, :], kS[:, s, :, :], mS[:, b, :, 1:CH + 1],
                                                                  ALU.subtract),
                                [M["msc", n], before("bsc", n - 1)], "km")
                M["ec", n] = op("act", lambda e: e.activation(q1[:, :, :], q1[:, :, :], ACT.Exp), [M["q1", n]], "ec")
                M["ed", n] = op("act", lambda e: e.activation(km[:, :, :], km[:, :, :], ACT.Exp), [M["km", n]], "ed")

            def b_sum(n):
                b, j = chunks[n]
                for g in range(2):
                    M["bsc", n] = op("dve", lambda e, g=g: e.tensor_tensor_scan(
                        BS[:, g, :], q1[:, g, :], km[:, g, :], Bc[:, b, g:g + 1], ALU.mult, ALU.add),
                        [M["ec", n], M["ed", n], before("Bc", n - 2), before("bS", n - 1), CST], "bsc")
                M["Bc", n] = op("dve", lambda e: e.tensor_copy(Bc[:, b, :], BS[:, :, CH - 1]), [M["bsc", n]], "Bc")
                M["lB", n] = op("act", lambda e: e.activation(BS[:, :, :], BS[:, :, :], ACT.Ln, bias=epsw[:, 0:1]),
                                [M["Bc", n], EPSM], "lB")
                c = None
                if j:
                    c = op("pool", lambda e: e.tensor_copy(bS[:, b, :, 0:1], bS[:, b, :, CH:CH + 1]),
                           [M["bS", n - 2], M["q2", n - 2]], "bSc")
                M["bS", n] = op("pool", lambda e: e.tensor_tensor(bS[:, b, :, 1:CH + 1], mS[:, b, :, 1:CH + 1],
                                                                  BS[:, :, :], ALU.add),
                                [M["lB", n], c, before("q2", n - 2), CST], "bS")

            def c_exps(n):
                b, j = chunks[n]
                s = n % 3
                for g in range(2):
                    M["q2", n] = op("dve", lambda e, g=g: e.scalar_tensor_tensor(
                        out=q2[:, g, :], in0=bS[:, b, g, 0:CH], scalar=wdec[:, g:g + 1], in1=kS[:, s, g, :],
                        op0=ALU.add, op1=ALU.subtract), [M["bS", n]], "q2")
                d = op("dve", lambda e: e.tensor_scalar(f[:, 0, :, :], q2[:, :, :], 0.0, None, ALU.min),
                       [M["q2", n]], "f0")
                x0 = op("act", lambda e: e.activation(f[:, 0, :, :], f[:, 0, :, :], ACT.Exp), [d], "x0")
                d = op("dve", lambda e: e.tensor_scalar(f[:, 1, :, :], q2[:, :, :], 0.0, None, ALU.max),
                       [M["q2", n]], "f1")
                x1 = op("act", lambda e: e.activation(f[:, 1, :, :], f[:, 1, :, :], ACT.Exp, scale=-1.0), [d], "x1")
                for g in range(2):
                    d = op("dve", lambda e, g=g: e.tensor_scalar(f[:, 3, g, :], q2[:, g, :], wu[:, g:g + 1], 0.0,
                                                                 ALU.subtract, ALU.max),
                           [M["q2", n], before("n2", n - 1)], "f3")
                x3 = op("act", lambda e: e.activation(f[:, 3, :, :], f[:, 3, :, :], ACT.Exp, scale=-1.0), [d], "x3")
                for g in range(2):
                    d = op("dve", lambda e, g=g: e.tensor_scalar(f[:, 2, g, :], q2[:, g, :], wu[:, g:g + 1], 0.0,
                                                                 ALU.subtract, ALU.min), [M["q2", n]], "f2")
                x2 = op("act", lambda e: e.activation(f[:, 2, :, :], f[:, 2, :, :], ACT.Exp), [d], "x2")
                M["x", n] = (x0, x1, x2, x3)
                M["evv", n] = op("pool", lambda e: e.tensor_tensor(f[:, 1, :, :], f[:, 1, :, :], vS[:, s, :, :],
                                                                   ALU.mult), [x1], "evv")
                M["n2", n] = op("pool", lambda e: e.tensor_tensor(n2[:, :, :], f[:, 3, :, :], vS[:, s, :, :],
                                                                  ALU.mult), [x3, before("num", n - 1)], "n2")

            def c_out(n):
                b, j = chunks[n]
                s, p = n % 3, n % 2
                x0, x1, x2, x3 = M["x", n]
                c = None
                if j:
                    c = op("dve", lambda e: e.tensor_copy(aS[:, b, :, 0:1], aS[:, b, :, CH:CH + 1]),
                           [M["asc", n - 2]], "asc0")
                for g in range(2):
                    M["asc", n] = op("dve", lambda e, g=g: e.tensor_tensor_scan(
                        aS[:, b, g, 1:CH + 1], f[:, 0, g, :], f[:, 1, g, :], aS[:, b, g, 0:1], ALU.mult, ALU.add),
                        [x0, M["evv", n], c, CST], "asc")
                n1 = op("dve", lambda e: e.tensor_tensor(q2[:, :, :], f[:, 2, :, :], aS[:, b, :, 0:CH], ALU.mult),
                        [x2, M["asc", n]], "n1")
                dn = op("dve", lambda e: e.scalar_tensor_tensor(
                    out=f[:, 2, :, :], in0=f[:, 2, :, :], scalar=epsw[:, 0:1], in1=f[:, 3, :, :],
                    op0=ALU.add, op1=ALU.add), [x3, EPSM], "dn")
                M["num", n] = op("dve", lambda e: e.tensor_tensor(q2[:, :, :], q2[:, :, :], n2[:, :, :], ALU.add),
                                 [n1, M["n2", n]], "num")
                ld = op("act", lambda e: e.activation(f[:, 2, :, :], f[:, 2, :, :], ACT.Ln), [dn], "ldn")
                rc = op("act", lambda e: e.activation(f[:, 2, :, :], f[:, 2, :, :], ACT.Exp, scale=-1.0), [ld], "rdn")
                ns = op("pool", lambda e: e.tensor_tensor(q2[:, :, :], q2[:, :, :], sg[:, s, :, :], ALU.mult),
                        [M["num", n], M["ev", n, 2]], "ns")
                M["rw", n] = op("dve", lambda e: e.tensor_tensor(rw[:, :, :], q2[:, :, :], f[:, 2, :, :], ALU.mult),
                                [ns, rc, before("str", n - 1)], "rw")
                for g in range(2):
                    M["bst", n] = op("dve", lambda e, g=g: e.bn_stats(bst[:, b, g, j, :], rw[:, g, :]),
                                     [M["rw", n]], "bst")
                M["str", n] = dma(rwkv_d[b, :, :, j * CH:(j + 1) * CH].rearrange("g p t -> p g t"), rw[:, :, :],
                                  [M["rw", n]], "str")

            N = len(chunks)
            load_x(0)
            load_x(1)
            LD1 = load_ffn_weights()
            for i in range(N + 2):
                if i < N:
                    a_norm(i)
                    a_turn(i)
                    if i + 2 < N:
                        load_x(i + 2)
                if 1 <= i <= N:
                    b_max(i - 1)
                if i >= 2:
                    c_exps(i - 2)
                if i < N:
                    a_mix(i)
                    a_rkv(i)
                if 1 <= i <= N:
                    b_sum(i - 1)
                if i >= 2:
                    c_out(i - 2)

            for b in range(NB):
                for g in range(2):
                    m = op("dve", lambda e, b=b, g=g: e.bn_aggr(
                        gmv[:, b, g, :], bst[:, b, g, :, :].rearrange("p j s -> p (j s)")), [M["bst", N - 1]], "gag")
            G1 = op("pe", lambda e: e.matmul(PS[:, 0, 0:4], grp[:, :], gmv[:, :, :, 0].rearrange("p b g -> p (b g)"),
                                             start=True, stop=True), [m, M["xT", N - 1], LD0], "g1")
            m = op("dve", lambda e: e.tensor_copy(gtm[:, :, :, 0], PS[:, 0, 0:4].rearrange("p (b g) -> p b g", b=2)),
                   [G1], "g2")
            m = op("dve", lambda e: e.tensor_tensor(gtm[:, :, :, 1], gmv[:, :, :, 0], gtm[:, :, :, 0], ALU.subtract),
                   [m], "g2")
            m = op("dve", lambda e: e.tensor_tensor(gtm[:, :, :, 2], gtm[:, :, :, 1], gtm[:, :, :, 1], ALU.mult),
                   [m], "g2")
            m = op("dve", lambda e: e.tensor_tensor(gtm[:, :, :, 3], gtm[:, :, :, 2], gmv[:, :, :, 1], ALU.add),
                   [m], "g2")
            G3 = op("pe", lambda e: e.matmul(PS[:, 1, 0:4], grp[:, :], gtm[:, :, :, 3].rearrange("p b g -> p (b g)"),
                                             start=True, stop=True), [m], "g1")
            m = op("dve", lambda e: e.tensor_scalar(gsc[:, :, :], PS[:, 1, 0:4].rearrange("p (b g) -> p b g", b=2),
                                                    EPS_LN, None, ALU.add), [G3], "g2")
            m = inv_sqrt(gsc[:, :, :].rearrange("p b g -> p (b g)"), m, "g4")
            for b in range(NB):
                m2 = op("dve", lambda e, b=b: e.tensor_tensor(gsc[:, b, :], gsc[:, b, :],
                                                              vecs[:, VEC["gamma"]:VEC["gamma"] + 2], ALU.mult),
                        [m], "g2")
            m = op("dve", lambda e: e.tensor_tensor(gtm[:, :, :, 1], gtm[:, :, :, 0], gsc[:, :, :], ALU.mult),
                   [m2], "g2")
            for b in range(NB):
                GN = op("dve", lambda e, b=b: e.tensor_tensor(gsh[:, b, :], vecs[:, VEC["beta"]:VEC["beta"] + 2],
                                                              gtm[:, b, :, 1], ALU.subtract), [m], "g2")
            STORED = [M["str", N - 1]]

        NY = 8
        shift = sb("shift", [2, 128])
        mask = sb("mask", [2, 256])
        qsks = sb("qsks", [2, 256])
        xin = sb("xin", [2, 256])
        rk = sb("rk", [2, 2, 128])
        nT = sb("nT", [2, 2, 128])
        x1 = sb("x1", [8, 256])
        st0 = sb("st0", [8])
        mv0 = sb("mv0", [2])
        r0 = sb("r0", [1])
        y = sb("y", [NY, 256])
        tb = sb("tb", [8, 256])
        rt = sb("rt", [2, 256])
        hT = sb("hT", [2, 2, 2, 129])
        sq = sb("sq", [1024])
        ss = sb("ss", [16])
        rs = sb("rs", [2, 16])
        sc = sb("sc", [2, 8])
        Ar = sb("Ar", [1024])
        Br = sb("Br", [1024])
        qT = sb("qT", [2, 4, 128])
        kT = sb("kT", [2, 2, 4, 128])
        vv = sb("vv", [2, 3, 8, 65])
        Sm = sb("Sm", [8, 256])
        mx = sb("mx", [2, 8])
        nb = sb("nb", [2, 8])
        PT = sb("PT", [4, 256])
        ro = sb("ro", [8])
        oS = sb("oS", [8, 64])
        oT = sb("oT", [4, 128])
        x2 = sb("x2", [2, 2, 256])
        st1 = sb("st1", [12])
        mv1 = sb("mv1", [2])
        r1 = sb("r1", [1])
        z = sb("z", [256])
        zT = sb("zT", [2, 128])
        Gl = sb("Gl", [6, 128])
        uT = sb("uT", [6, 128])
        os_ = sb("os", [2, 256])

        END = [op("dve", lambda e: e.memset(vv[:, :, :, :, 64:65], 1.0), [GN] + STORED, "end"),
               op("dve", lambda e: e.memset(hT[:, :, 1, 0, 0:1], 0.0), [], "end"),
               op("dve", lambda e: e.memset(hT[:, :, 0, 1, 0:1], 0.0), [], "end")]
        END = op("dve", lambda e: e.memset(uT[0:64, 5, :], 1.0), [], "end")
        for eng in ("pe", "act", "pool", "sp"):
            op(eng, None, [END])
        dma(shift[:, :, :], shift_d, [END], "ld2")
        dma(mask[:, :, :], mask_d, [END], "ld2")
        LD2 = dma(qsks[:, :, :], qsk, [END], "ld2")
        for eng in ("pe", "act", "dve", "pool"):
            op(eng, None, [LD1, LD2])

        M = {}

        def before(name, n, *rest):
            return M[(name, n, *rest)] if n >= 0 else None

        units = []
        for step in range(NG + LAG):
            if step < NG:
                units.append((step, 0))
            if step >= LAG:
                units.append((step - LAG, 1))
        pos = {u: n for n, u in enumerate(units)}
        U = len(units)

        def first_win(g):
            return g % NWIN == 0

        def loads(g):
            b, w = divmod(g, NWIN)
            M["lxi", g] = dma(xin[:, g % 2, :], x[b, w * 128:(w + 1) * 128, :], [before("x1", g - 2)], f"lxi{g % 2}")
            M["lrk", g] = dma(rk[:, g % 2, :, :], rwkv_d[b, :, :, w * 128:(w + 1) * 128].rearrange("g p t -> p g t"),
                              [before("nT", g - 2)] + STORED, f"lrk{g % 2}")
            M["ltb", g] = dma(tb[:, g % 8, :], tab[w * 128:(w + 1) * 128, :], [before("rt", g - 8, 1)], f"ltb{g % 8}")

        def pre_norm(g):
            b = g // NWIN
            for c in range(2):
                M["nT", g] = op("pool", lambda e, c=c: e.tensor_scalar(
                    nT[:, g % 2, c, :], rk[:, g % 2, c, :], gsc[:, b, c:c + 1], gsh[:, b, c:c + 1],
                    ALU.mult, ALU.add), [M["lrk", g], before("p0", g - 2), GN], "nT")

        def pre_mm(g):
            for c in range(2):
                M["p0", g] = op("pe", lambda e, c=c: e.matmul(
                    PS[:, 1, 0:256], nT[:, g % 2, c, :], Wr[:, 3, c, :], start=(c == 0), stop=(c == 1)),
                    [M["nT", g], M.get("kTe")], "p0" if c else None)

        def pre_y(g):
            s = g % 8
            M["x1", g] = M["b1"] = op("dve", lambda e: e.tensor_tensor(x1[:, s, :], PS[:, 1, 0:256], xin[:, g % 2, :],
                                                                       ALU.add), [M["p0", g], M["lxi", g]], "x1")
            a = op("dve", lambda e: e.bn_stats(st0[:, 0:6], x1[:, s, :]), [M["x1", g]], "ps")
            a = op("dve", lambda e: e.bn_aggr(mv0[:, :], st0[:, 0:6]), [a], "ps")
            a = op("dve", lambda e: e.tensor_scalar(r0[:, :], mv0[:, 1:2], EPS_LN, None, ALU.add), [a], "ps")
            a = inv_sqrt(r0[:, :], a, "r0")
            M["y", g, 0] = op("dve", lambda e: e.tensor_scalar(
                y[:, pos[g, 0] % NY, :], x1[:, s, :], mv0[:, 0:1], r0[:, 0:1], ALU.subtract, ALU.mult), [a], "y0")

        def a_rt(g, l):
            n = pos[g, l]
            M["rt", g, l] = op("pool", lambda e: e.tensor_tensor(rt[:, n % 2, :], tb[:, g % 8, :], qsks[:, l, :],
                                                                 ALU.mult),
                               [M["ltb", g], before("rope", n - 2)], "rt")

        def a_hT(g, l):
            n = pos[g, l]
            for c in range(2):
                M["p1", n] = op("pe", lambda e, c=c: e.transpose(
                    PS[:, 0, c * 128:(c + 1) * 128], y[:, n % NY, c * 128:(c + 1) * 128], ident[:, :]),
                    [M["y", g, l], M.get("qTe")], "p1" if c else None)
            h = hT[:, l, g % 2, :, :]
            M["hT", n] = op("act", lambda e: e.activation(h[:, :, 1:129],
                                                          PS[:, 0, 0:256].rearrange("p (c t) -> p c t", c=2), ACT.Copy),
                            [M["p1", n]], "hT")
            nxt = hT[:, l, (g + 1) % 2, 1, 0:1]
            if first_win(g + 1):
                M["hTc", g, l] = op("act", lambda e: e.activation(nxt, PS[:, 0, 255:256], ACT.Copy, scale=0.0),
                                    [M["p1", n]], "hTc")
            else:
                M["hTc", g, l] = op("act", lambda e: e.activation(nxt, PS[:, 0, 255:256], ACT.Copy),
                                    [M["p1", n]], "hTc")

        def a_qkv(g, l):
            n = pos[g, l]
            for i, bank in ((1, 1), (0, 0), (2, 2)):
                for c in range(2):
                    M["p2", n, i] = op("pe", lambda e, i=i, bank=bank, c=c: e.matmul(
                        PS[:, bank, :], hT[:, l, g % 2, c, 1 - c:129 - c], WQ[:, l, c, i * 512:(i + 1) * 512],
                        start=(c == 0), stop=(c == 1)),
                        [M["hT", n], M["hTc", g, l], (M.get("kTe"), M.get("qTe"), M.get("mlpA"))[1 - i if i < 2 else 2],
                         M.get("b1") if i == 1 else None], f"p2{i}" if c else None)

        def a_square(g, l):
            n = pos[g, l]
            for i in (1, 0):
                M["sq", n, i] = op("act", lambda e, i=i: e.activation(sq[:, i * 512:(i + 1) * 512], PS[:, i, :],
                                                                      ACT.Square),
                                   [M["p2", n, i], before("ss", n - 1)], f"sq{i}")

        def a_v(g, l):
            n = pos[g, l]
            M["v", g, l] = op("act", lambda e: e.activation(
                vv[:, l, g % 3, :, 0:64], PS[:, 2, :].rearrange("p (h d) -> p h d", h=8), ACT.Copy),
                [M["p2", n, 2]], "v")

        def a_rope(g, l):
            n = pos[g, l]
            for i in (1, 0):
                X = PS[:, i, :].rearrange("p (h d) -> p h d", h=8)
                A = Ar[:, i * 512:(i + 1) * 512].rearrange("p (h d) -> p h d", h=8)
                B = Br[:, i * 512:(i + 1) * 512].rearrange("p (h d) -> p h d", h=8)
                t0 = rt[:, n % 2, i * 128:i * 128 + 64].unsqueeze(1)
                t1 = rt[:, n % 2, i * 128 + 64:i * 128 + 128].unsqueeze(1)
                ws = [M["sq", n, i], M["rt", g, l], before("p3", n - 1)]
                op("dve", lambda e, X=X, A=A, t0=t0: e.tensor_tensor(A, X, t0.broadcast_to([128, 8, 64]), ALU.mult),
                   ws)
                op("dve", lambda e, X=X, B=B, t1=t1: e.tensor_tensor(
                    B[:, :, 0:32], X[:, :, 32:64], t1[:, :, 0:32].broadcast_to([128, 8, 32]), ALU.mult), ws)
                M["rope", n, i] = op("dve", lambda e, X=X, B=B, t1=t1: e.tensor_tensor(
                    B[:, :, 32:64], X[:, :, 0:32], t1[:, :, 32:64].broadcast_to([128, 8, 32]), ALU.mult), ws, "rope")
            M["rope", n] = M["rope", n, 0]

        def a_scales(g, l):
            n = pos[g, l]
            M["ss", n] = op("dve", lambda e: e.tensor_reduce(
                ss[:, :], sq[:, :].rearrange("p (h d) -> p h d", h=16), AX_X, ALU.add),
                [M["sq", n, 0], M["sq", n, 1]], "ss")
            a = op("dve", lambda e: e.tensor_scalar(rs[:, n % 2, :], ss[:, :], 1e-24, None, ALU.max),
                   [M["ss", n], before("kn", n - 2)], "rsm")
            M["rs", n] = inv_sqrt(rs[:, n % 2, :], a, "rs")
            M["sc", n] = op("dve", lambda e: e.tensor_scalar(sc[:, n % 2, :], rs[:, n % 2, 0:8], 8.0, None, ALU.mult),
                            [M["rs", n]], "sc")

        def a_rot(g, l):
            n = pos[g, l]
            k = op("pool", lambda e: e.tensor_tensor(Ar[:, 512:1024], Ar[:, 512:1024], Br[:, 512:1024], ALU.add),
                   [M["rope", n, 1]], "kr")
            A = Ar[:, 512:1024].rearrange("p (h d) -> p h d", h=8)
            M["kn", n] = op("pool", lambda e: e.tensor_tensor(
                A, A, rs[:, n % 2, 8:16].unsqueeze(2).broadcast_to([128, 8, 64]), ALU.mult), [k, M["rs", n]], "kn")
            M["qr", n] = op("pool", lambda e: e.tensor_tensor(Ar[:, 0:512], Ar[:, 0:512], Br[:, 0:512], ALU.add),
                            [M["rope", n, 0]], "qr")

        def a_qkT(g, l):
            n = pos[g, l]
            for i, src in ((1, "kn"), (0, "qr")):
                for c in range(4):
                    M["p3", n] = M["p3", n, i] = op("pe", lambda e, i=i, c=c: e.transpose(
                        PS[:, i, c * 128:(c + 1) * 128], Ar[:, i * 512 + c * 128:i * 512 + (c + 1) * 128], ident[:, :]),
                        [M[src, n], M["rope", n, 0]], "p3" if c == 3 else None)

        def a_qT(g, l):
            n = pos[g, l]
            M["qTe"] = M["qT", n] = op("act", lambda e: e.activation(
                qT[:, n % 2, :, :].rearrange("p c t -> p (c t)"), PS[:, 0, :], ACT.Copy), [M["p3", n, 0]], "qT")

        def a_kT(g, l):
            n = pos[g, l]
            M["kTe"] = M["kT", g, l] = op("dve", lambda e: e.tensor_copy(
                kT[:, l, g % 2, :, :].rearrange("p c t -> p (c t)"), PS[:, 1, :]), [M["p3", n, 1]], "kT")

        def cols(g):
            return (g % 2 * 128, g % 2 * 128 + 128) if first_win(g) else (0, 256)

        def b_scores(g, l, q):
            n = pos[g, l]
            c0, c1 = cols(g)
            for h in range(4 * q, 4 * q + 4):
                p0 = 64 * (h % 2)
                dst = PS[:, 3 + h % 2, (h // 2 % 2) * 256 + c0:(h // 2 % 2) * 256 + c1]
                if first_win(g):
                    rhs = kT[p0:p0 + 64, l, g % 2, h // 2, :]
                else:
                    rhs = kT[p0:p0 + 64, l, :, h // 2, :]
                M["p4", n, h] = op("pe", lambda e, dst=dst, rhs=rhs, p0=p0, h=h: e.matmul(
                    dst, qT[p0:p0 + 64, n % 2, h // 2, :], rhs, start=True, stop=True),
                    [M["qT", n], M["kT", g, l], M.get("ptA"), M.get("ptD")], "p4")

        def b_max(g, l, q):
            n = pos[g, l]
            c0, c1 = cols(g)
            for h in range(4 * q, 4 * q + 4):
                M["mx", n, q] = op("dve", lambda e, h=h: e.tensor_tensor_reduce(
                    Sm[:, h, c0:c1], PS[:, 3 + h % 2, (h // 2 % 2) * 256 + c0:(h // 2 % 2) * 256 + c1],
                    mask[:, g % 2, c0:c1], 1.0, -3.0e38, ALU.add, ALU.max, mx[:, n % 2, h:h + 1]),
                    [M["p4", n, 4 * q + 3], before("p5", n - 1, q)], "mx")
            M["nb", n, q] = op("dve", lambda e: e.scalar_tensor_tensor(
                out=nb[:, n % 2, 4 * q:4 * q + 4], in0=mx[:, n % 2, 4 * q:4 * q + 4], scalar=-1.0,
                in1=sc[:, n % 2, 4 * q:4 * q + 4], op0=ALU.mult, op1=ALU.mult), [M["mx", n, q], M["sc", n]], "nb")

        def b_exp(g, l, q):
            n = pos[g, l]
            c0, c1 = cols(g)
            for h in range(4 * q, 4 * q + 4):
                M["ex", n, q] = M["ex", n, q, h % 4] = op("act", lambda e, h=h: e.activation(
                    Sm[:, h, c0:c1], Sm[:, h, c0:c1], ACT.Exp, bias=nb[:, n % 2, h:h + 1],
                    scale=sc[:, n % 2, h:h + 1]), [M["nb", n, q]], "ex")

        def b_turn(g, l, q):
            n = pos[g, l]
            sides = [g % 2] if first_win(g) else [0, 1]
            for i in range(4):
                h = 4 * q + i
                for s in sides:
                    M["p5", n, q] = M["p5", n, q, i // 2] = op("pe", lambda e, h=h, s=s, i=i: e.transpose(
                        PS[:, 3 + i // 2, (i % 2) * 256 + s * 128:(i % 2) * 256 + s * 128 + 128],
                        Sm[:, h, s * 128:(s + 1) * 128], ident[:, :]),
                        [M["ex", n, q, i], M["mx", n, q]], "p5" if i % 2 and s == sides[-1] else None)

        def b_pt(g, l, q, i, eng):
            n = pos[g, l]
            c0, c1 = cols(g)
            src = PS[:, 3 + i, :].rearrange("p (h j) -> p h j", h=2)[:, :, c0:c1]
            dst = PT[:, 2 * i:2 * i + 2, c0:c1]
            ws = [M["p5", n, q, i], M.get("pv")]
            if eng == "act":
                m = op("act", lambda e: e.activation(dst, src, ACT.Copy), ws, "ptA")
                M["ptA"] = m
            else:
                m = op("dve", lambda e: e.tensor_copy(dst, src), ws, "ptD")
                M["ptD"] = m

        def b_pv(g, l, q):
            n = pos[g, l]
            sides = [g % 2] if first_win(g) else [0, 1]
            for i in range(4):
                h = 4 * q + i
                for s in sides:
                    gv = g if s == g % 2 else g - 1
                    M["pv"] = M["p6", n, q] = op("pe", lambda e, h=h, i=i, s=s, gv=gv: e.matmul(
                        PS[:, 5, 65 * i:65 * i + 65], PT[:, i, s * 128:(s + 1) * 128], vv[:, l, gv % 3, h, :],
                        start=(s == sides[0]), stop=(s == sides[-1])),
                        [M["ptA"], M["ptD"], M["v", g, l], M.get("on")],
                        "p6" if i == 3 and s == sides[-1] else None)

        def b_norm(g, l, q):
            n = pos[g, l]
            O = PS[:, 5, 0:260].rearrange("p (h d) -> p h d", h=4)
            a = op("dve", lambda e: e.reciprocal(ro[:, 4 * q:4 * q + 4], O[:, :, 64]), [M["p6", n, q]], "ro")
            M["on"] = M["on", n, q] = op("dve", lambda e: e.tensor_tensor(
                oS[:, 4 * q:4 * q + 4, :], O[:, :, 0:64],
                ro[:, 4 * q:4 * q + 4].unsqueeze(2).broadcast_to([128, 4, 64]), ALU.mult),
                [a, before("p7", n - 1)], "on")

        def c_oT(g, l):
            n = pos[g, l]
            for c in range(4):
                M["p7", n] = op("pe", lambda e, c=c: e.transpose(
                    PS[:, 7, c * 128:(c + 1) * 128], oS[:, 2 * c:2 * c + 2, :].rearrange("p h d -> p (h d)"),
                    ident[:, :]), [M["on", n, 1], M.get("x3")], "p7" if c == 3 else None)
            M["oT", n] = op("act", lambda e: e.activation(oT[:, :, :].rearrange("p c t -> p (c t)"), PS[:, 7, :],
                                                          ACT.Copy), [M["p7", n]], "oT")

        def c_wo(g, l):
            n = pos[g, l]
            for c in range(4):
                M["p8", n] = op("pe", lambda e, c=c: e.matmul(PS[:, 7, 0:256], oT[:, c, :], WO[:, l, c, :],
                                                              start=(c == 0), stop=(c == 3)),
                                [M["oT", n]], "p8" if c == 3 else None)

        def c_x2(g, l):
            n = pos[g, l]
            M["x2", g, l] = op("dve", lambda e: e.tensor_tensor(x2[:, l, g % 2, :], PS[:, 7, 0:256], y[:, n % NY, :],
                                                                ALU.add), [M["p8", n], M["y", g, l]], "x2")

        def c_shift(g, l):
            n = pos[g, l]
            one = first_win(g)
            M["p9", n] = op("pe", lambda e: e.matmul(PS[:, 7, 0:128], shift[:, 0, :], x2[:, l, g % 2, 128:256],
                                                     start=True, stop=one), [M["x2", g, l]], "p9" if one else None)
            if not one:
                M["p9", n] = op("pe", lambda e: e.matmul(PS[:, 7, 0:128], shift[:, 1, :],
                                                         x2[:, l, (g - 1) % 2, 128:256], start=False, stop=True),
                                [], "p9")

        def c_ln(g, l):
            n = pos[g, l]
            op("dve", lambda e: e.bn_stats(st1[:, 0:6], x2[:, l, g % 2, 0:128]), [M["x2", g, l]])
            a = op("dve", lambda e: e.bn_stats(st1[:, 6:12], PS[:, 7, 0:128]), [M["p9", n]], "ls")
            a = op("dve", lambda e: e.bn_aggr(mv1[:, :], st1[:, :]), [a], "ls")
            a = op("dve", lambda e: e.tensor_scalar(r1[:, :], mv1[:, 1:2], EPS_LN, None, ALU.add), [a], "ls")
            a = inv_sqrt(r1[:, :], a, "r1")
            op("dve", lambda e: e.tensor_scalar(z[:, 0:128], x2[:, l, g % 2, 0:128], mv1[:, 0:1], r1[:, 0:1],
                                                ALU.subtract, ALU.mult), [a])
            M["z", n] = op("dve", lambda e: e.tensor_scalar(z[:, 128:256], PS[:, 7, 0:128], mv1[:, 0:1], r1[:, 0:1],
                                                            ALU.subtract, ALU.mult), [a], "z")

        def c_zT(g, l):
            n = pos[g, l]
            for c in range(2):
                M["p10", n] = op("pe", lambda e, c=c: e.transpose(PS[:, 7, c * 128:(c + 1) * 128],
                                                                  z[:, c * 128:(c + 1) * 128], ident[:, :]),
                                 [M["z", n]], "p10" if c else None)

        def c_zTe(g, l):
            n = pos[g, l]
            for c in range(2):
                M["zT", n] = op("act", lambda e, c=c: e.activation(
                    zT[:, c, :], PS[:, 7, c * 128:(c + 1) * 128], ACT.Identity, bias=V("lb", 2 * l + c),
                    scale=V("lg", 2 * l + c)), [M["p10", n]], "zT")

        def c_w1(g, l, part):
            n = pos[g, l]
            ch = [(6, j * 128, 640 + j * 128, 128) for j in range(4)] + [(2, j * 128, j * 128, 128) for j in range(4)] \
                if part == 0 else [(2, 128, 1280, 106), (6, 0, 640 + 512, 128), (2, 0, 512, 128)]
            for bank, o, wcol, m in ch:
                for c in range(2):
                    M["p11", n, part] = op("pe", lambda e, bank=bank, o=o, wcol=wcol, m=m, c=c: e.matmul(
                        PS[0:m, bank, o:o + 128], W1[:, l, c, wcol:wcol + m], zT[:, c, :],
                        start=(c == 0), stop=(c == 1)),
                        [M["zT", n], M["v", g, l], M.get("latest_v"), M.get("mlpA"), M.get("mlpG")],
                        "p11" if c else None)
                M["p11", n, bank, o, part] = M["p11", n, part]

        def c_gelu(g, l, part):
            n = pos[g, l]
            for j in ([0, 1, 2, 3] if part == 0 else [5, 4]):
                lo, hi = (64, 64 + TAIL) if j == 5 else (0, 128)
                src = PS[lo:hi, 2, 128:256] if j == 5 else PS[:, 6, j % 4 * 128:j % 4 * 128 + 128]
                bi = vecs[lo:hi, VEC["b1g"] + 6 * l + j:VEC["b1g"] + 6 * l + j + 1]
                M["gl", n, j] = op("act", lambda e, lo=lo, hi=hi, src=src, bi=bi, j=j: e.activation(
                    Gl[lo:hi, j, :], src, ACT.Gelu, bias=bi),
                    [M["p11", n, part], before("u", n - 1)], "gl")
            M["mlpG"] = M["gl", n, j]

        def c_glu(g, l, part):
            n = pos[g, l]
            for j in ([0, 1, 2, 3] if part == 0 else [5, 4]):
                if j == 5:
                    s, w, gl = PS[0:TAIL, 2, 128:256], TAIL, Gl[64:64 + TAIL, 5, :]
                else:
                    s, w, gl = PS[:, 2, j % 4 * 128:j % 4 * 128 + 128], 128, Gl[:, j, :]
                bi = vecs[0:w, VEC["b1a"] + 6 * l + j:VEC["b1a"] + 6 * l + j + 1]
                M["u", n] = op("dve", lambda e, s=s, w=w, gl=gl, bi=bi, j=j: e.scalar_tensor_tensor(
                    out=uT[0:w, j, :], in0=s, scalar=bi, in1=gl, op0=ALU.add, op1=ALU.mult),
                    [M["p11", n, part], M["gl", n, 4 if part else j]], "u")
            M["mlpA"] = M["u", n]

        def c_w2(g, l):
            n = pos[g, l]
            for j in range(6):
                k = 128 if j < 5 else TAIL + 1
                M["p12", n] = op("pe", lambda e, j=j, k=k: e.matmul(
                    PS[:, 7, 0:256], uT[0:k, j, :], W2[0:k, l, j, :], start=(j == 0), stop=(j == 5)),
                    [M["u", n]], "p12" if j == 5 else None)

        def c_x3(g, l):
            n = pos[g, l]
            b, w = divmod(g, NWIN)
            if l == 0:
                M["x3"] = M["y", g, 1] = op("dve", lambda e: e.tensor_tensor(
                    y[:, pos[g, 1] % NY, :], PS[:, 7, 0:256], x2[:, l, g % 2, :], ALU.add), [M["p12", n]], "x3")
                return
            a = M["x3"] = op("dve", lambda e: e.tensor_tensor(os_[:, g % 2, :], PS[:, 7, 0:256], x2[:, l, g % 2, :],
                                                              ALU.add),
                             [M["p12", n], before("st", g - 2)], "x3")
            a = op("dve", lambda e: e.tensor_tensor(os_[:, g % 2, :], os_[:, g % 2, :], x1[:, g % 8, :], ALU.add),
                   [a], "os")
            M["st", g] = dma(out[b, w * 128:(w + 1) * 128, :], os_[:, g % 2, :], [a], f"st{g % 2}")

        for g in range(2):
            loads(g)
        pre_at = {pos[g, 0] - 1: g for g in range(NG)}
        for t in range(-1, U + 2):
            al = units[t] if 0 <= t < U else None
            be = units[t - 1] if 0 <= t - 1 < U else None
            ga = units[t - 2] if 0 <= t - 2 < U else None
            pg = pre_at.get(t)
            if pg is not None:
                pre_norm(pg)
            if al:
                a_rt(*al)
                a_hT(*al)
            if pg is not None:
                pre_mm(pg)
                pre_y(pg)
                if pg + 2 < NG:
                    loads(pg + 2)
            if be:
                b_scores(*be, 0)
                b_max(*be, 0)
                b_exp(*be, 0)
            if ga:
                c_oT(*ga)
            if al:
                a_qkv(*al)
                a_square(*al)
                a_v(*al)
                M["latest_v"] = M["v", al[0], al[1]]
                a_rope(*al)
                a_scales(*al)
                a_rot(*al)
            if ga:
                c_wo(*ga)
                c_x2(*ga)
            if be:
                b_turn(*be, 0)
                b_pt(*be, 0, 0, "act")
                b_pt(*be, 0, 1, "dve")
            if ga:
                c_shift(*ga)
                c_ln(*ga)
            if be:
                b_pv(*be, 0)
                b_norm(*be, 0)
                b_scores(*be, 1)
                b_max(*be, 1)
            if ga:
                c_zT(*ga)
                c_zTe(*ga)
            if be:
                b_exp(*be, 1)
            if ga:
                c_w1(*ga, 0)
                c_gelu(*ga, 0)
                c_glu(*ga, 0)
            if be:
                b_turn(*be, 1)
                b_pt(*be, 1, 0, "act")
                b_pt(*be, 1, 1, "dve")
            if al:
                a_qkT(*al)
                a_qT(*al)
                a_kT(*al)
            if ga:
                c_w1(*ga, 1)
                c_gelu(*ga, 1)
                c_glu(*ga, 1)
            if be:
                b_pv(*be, 1)
                b_norm(*be, 1)
            if ga:
                c_w2(*ga)
                c_x3(*ga)
        op("sp", None, [M["st", NG - 1], M["st", NG - 2]])

        block = ctx.enter_context(nc.Block())

        @block.sync
        def _(e):
            Q.run("sp", e)

        @block.tensor
        def _(e):
            Q.run("pe", e)

        @block.scalar
        def _(e):
            Q.run("act", e)

        @block.vector
        def _(e):
            Q.run("dve", e)

        @block.gpsimd
        def _(e):
            Q.run("pool", e)


def constants():
    f = np.float32
    half = np.arange(0, 64, 2, dtype=f)
    inv = (f(1.0) / np.power(f(10000.0), half / f(64))).astype(f)
    t = np.arange(T, dtype=f)
    fr = t[:, None] * inv[None, :]
    fr = np.concatenate([fr, fr], -1).astype(np.float64)
    base = ((half + f(0.4 * 64)) / f(1.4 * 64)).astype(f)
    power = ((t - f(T // 2)) / f(64.0)).astype(f)
    scale = base.astype(np.float64)[None, :] ** power.astype(np.float64)[:, None]
    scale = np.concatenate([scale, scale], -1)
    sgn = np.concatenate([-np.ones(32), np.ones(32)])[None, :]
    cos, sin = np.cos(fr), np.sin(fr) * sgn
    tab = np.concatenate([cos * scale, sin * scale, cos / scale, sin / scale], -1).astype(f)
    ident = np.eye(128, dtype=f)
    shift = np.zeros((128, 2, 128), f)
    for i in range(127):
        shift[i, 0, i + 1] = 1.0
    shift[127, 1, 0] = 1.0
    grp = np.kron(np.eye(8), np.full((16, 16), 1.0 / 16)).astype(f)
    i, j = np.arange(128)[:, None], np.arange(128)[None, :]
    cur = np.where(i >= j, 0.0, MASKED)
    prv = np.where(i <= j, 0.0, MASKED)
    mask = np.zeros((128, 2, 256), f)
    mask[:, 0, 0:128], mask[:, 0, 128:256] = cur, prv
    mask[:, 1, 128:256], mask[:, 1, 0:128] = cur, prv
    return tab, ident, shift, grp, mask


def kernel(**inputs):
    import numpy as _np
    import concourse.bacc as _bacc
    from concourse import mybir as _mybir
    from concourse.bass_utils import run_bass_kernel_spmd as _run

    a = {k: _np.asarray(v) for k, v in inputs.items()}

    def per_partition(v):
        return v.reshape(-1, 128).T

    vec = _np.zeros((128, NVEC), _np.float32)
    for name, key in (("mix_r", "L0_attn_time_mix_r"), ("mix_k", "L0_attn_time_mix_k"),
                      ("mix_v", "L0_attn_time_mix_v"), ("decay", "L0_attn_time_decay"),
                      ("first", "L0_attn_time_first"), ("gamma", "L0_attn_ln_gamma"), ("beta", "L0_attn_ln_beta")):
        vec[:, VEC[name]:VEC[name] + 2] = per_partition(a[key].reshape(-1))
    vec[:, VEC["lg"]:VEC["lg"] + 4] = per_partition(a["L0_ffn_ln_g"].reshape(-1))
    vec[:, VEC["lb"]:VEC["lb"] + 4] = per_partition(a["L0_ffn_ln_b"].reshape(-1))
    for l in range(2):
        b1 = a["L0_ffn_b1"][l]
        for name, o, row in (("b1a", 0, 0), ("b1g", HID, 64)):
            c = VEC[name] + 6 * l
            vec[:, c:c + 5] = per_partition(b1[o:o + 640])
            vec[row:row + TAIL, c + 5] = b1[o + 640:o + HID]
    qs, ks = a["L0_ffn_q_scale"], a["L0_ffn_k_scale"]
    row = _np.concatenate([qs, _np.roll(qs, 32, 1), ks, _np.roll(ks, 32, 1)], 1)
    qsk = _np.ascontiguousarray(_np.broadcast_to(row[None], (128, 2, 256)))
    wrkvo = _np.stack([a["L0_attn_W_" + n].T for n in "rkvo"])
    tab, ident, shift, grp, mask = constants()
    arrays = {"x": a["L0_attn_x"], "wrkvo": wrkvo, "wqkv": a["L0_ffn_wqkv"], "wo": a["L0_ffn_wo"],
              "w1": a["L0_ffn_w1"], "w2": a["L0_ffn_w2"], "b2": a["L0_ffn_b2"], "vec": vec, "qsk": qsk, "tab": tab,
              "ident_d": ident, "shift_d": shift, "grp_d": grp, "mask_d": mask}
    arrays = {k: _np.ascontiguousarray(v) for k, v in arrays.items()}
    nc = _bacc.Bacc("TRN2", target_bir_lowering=False, num_devices=1)
    args = {k: nc.dram_tensor(k, v.shape, _mybir.dt.from_np(v.dtype), kind="ExternalInput").ap()
            for k, v in arrays.items()}
    o = nc.dram_tensor("out_dram", (NB, T, C), _mybir.dt.float32, kind="ExternalOutput").ap()
    build(nc, out=o, **args)
    r = _run(nc, [arrays], core_ids=[0])
    return r.results[0]["out_dram"]
```

```python
from contextlib import ExitStack

import numpy as np
import concourse.bass as bass
from concourse import mybir

F32 = mybir.dt.float32
F32R = mybir.dt.float32r
ALU = mybir.AluOpType
ACT = mybir.ActivationFunctionType
AX_X = mybir.AxisListType.X

NB = 2
T = 4096
NWIN = T // 128
NG = NB * NWIN
C = 256
CH = 512
NCH = T // CH
HID = 682
TAIL = HID - 5 * 128
LOW = -1.0e38
MASKED = -1.0e30
EPS_W = 1e-8
EPS_LN = 1e-5

VEC = {"mix_r": 0, "mix_k": 2, "mix_v": 4, "decay": 6, "first": 8, "gamma": 10, "beta": 12,
       "lg": 14, "lb": 18, "b1a": 22, "b1g": 34}
NVEC = 46


class Queues:

    def __init__(self, nc, ctx):
        self.nc, self.ctx = nc, ctx
        self.sems, self.count = {}, {}
        self.q = {"pe": [], "act": [], "dve": [], "pool": [], "sp": []}

    def op(self, eng, fn, waits=(), sig=None, by=1):
        mark = None
        if sig is not None:
            if sig not in self.sems:
                self.sems[sig] = self.ctx.enter_context(self.nc.semaphore(sig))
                self.count[sig] = 0
            self.count[sig] += by
            mark = (sig, self.count[sig])
        self.q[eng].append((fn, [w for w in waits if w is not None], sig, by))
        return mark

    def run(self, eng, e):
        seen = {}
        for fn, waits, sig, by in self.q[eng]:
            for s, v in waits:
                if seen.get(s, 0) < v:
                    e.wait_ge(self.sems[s], v)
                    seen[s] = v
            if fn is None:
                continue
            ins = fn(e)
            if sig is not None:
                ins.then_inc(self.sems[sig], by)


def build(nc, x, wrkvo, wqkv, wo, w1, w2, b2, vec, qsk, tab, ident_d, grp_d, mask_d, out):
    ctx = ExitStack()
    with ctx:
        Q = Queues(nc, ctx)
        op = Q.op
        rwkv_d = nc.dram_tensor("rwkv_scratch", (NB, 2, 128, T), F32, kind="Internal").ap()
        x1_d = nc.dram_tensor("x1_scratch", (NB, T, C), F32, kind="Internal").ap()
        y_d = nc.dram_tensor("y_scratch", (NB, T, C), F32, kind="Internal").ap()

        def sb(name, shape, c=ctx, dt=F32):
            return c.enter_context(nc.sbuf_tensor(name, [128] + shape, dt))

        def pair(name, shape):
            return [sb(name + p, shape, dt=F32R) for p in "hl"]

        def weight_scratch(name, shape):
            return [nc.dram_tensor(name + p, tuple([128] + shape), F32, kind="Internal").ap() for p in "hl"]

        wq_d = weight_scratch("wq_scratch", [2, 1536])
        wo_d = weight_scratch("wo_scratch", [4, 256])
        w1_d = weight_scratch("w1_scratch", [2, 1386])
        w2_d = weight_scratch("w2_scratch", [6, 256])

        PS = ctx.enter_context(nc.psum_tensor("ps", [128, 8, 512], F32))

        ident = sb("ident", [128])
        vecs = sb("vecs", [NVEC])
        Wp = sb("Wp", [2, 256])
        WQ = pair("WQ", [2, 1536])
        WO = pair("WO", [4, 256])
        W1 = pair("W1", [2, 1386])
        W2 = pair("W2", [6, 256])
        wdec = sb("wdec", [2])
        wu = sb("wu", [2])
        epsw = sb("epsw", [1])
        mhalf = sb("mhalf", [16])
        gsc = sb("gsc", [NB, 2])
        gsh = sb("gsh", [NB, 2])

        def V(name, i):
            return vecs[:, VEC[name] + i:VEC[name] + i + 1]

        def dma(dst, src, waits, sig):
            return op("sp", lambda e: e.dma_start(dst, src), waits, sig, 16)

        dma(ident[:, :], ident_d, [], "ld0")
        dma(vecs[:, :], vec, [], "ld0")
        LD0 = dma(Wp[:, :, :], wrkvo[3].rearrange("(k p) n -> p k n", p=128), [], "ld0")

        MH = op("pool", lambda e: e.memset(mhalf[:, :], -0.5), [], "mh")

        def inv_sqrt(ap, src, sig):
            w = ap.shape[-1]
            return op("pool", lambda e: e.tensor_tensor(ap, ap, mhalf[:, 0:w], ALU.pow), [src, MH], sig)

        EPSM = op("dve", lambda e: e.memset(epsw[:, :], EPS_W), [], "cst")
        m = op("act", lambda e: e.activation(wdec[:, :], vecs[:, VEC["decay"]:VEC["decay"] + 2], ACT.Exp),
               [LD0], "wdec_e")
        m = op("dve", lambda e: e.tensor_scalar(wdec[:, :], wdec[:, :], -1.0, None, ALU.mult), [m, LD0], "wdec")
        WU = op("dve", lambda e: e.tensor_tensor(wu[:, :], wdec[:, :], vecs[:, VEC["first"]:VEC["first"] + 2],
                                                 ALU.add), [m], "wdec")

        with ExitStack() as c1:
            xc = sb("xc", [2, 4, 256], c1)
            mvs = sb("mvs", [4, 8], c1)
            mva = sb("mva", [4, 2], c1)
            rsd = sb("rsd", [4], c1)
            xT = sb("xT", [NB, 2, CH + 1], c1)
            dx = sb("dx", [2, CH], c1)
            xm = sb("xm", [2, 2, CH], c1)
            kS = sb("kS", [3, 2, CH], c1)
            vS = sb("vS", [3, 2, CH], c1)
            sg = sb("sg", [3, 2, CH], c1)
            mS = sb("mS", [NB, 2, CH + 1], c1)
            bS = sb("bS", [NB, 2, CH + 1], c1)
            aS = sb("aS", [NB, 2, CH + 1], c1)
            Bc = sb("Bc", [NB, 2], c1)
            q1 = sb("q1", [2, CH], c1)
            km = sb("km", [2, CH], c1)
            BS = sb("BS", [2, CH], c1)
            q2 = sb("q2", [2, CH], c1)
            f = sb("f", [4, 2, CH], c1)
            n2 = sb("n2", [2, CH], c1)
            rw = sb("rw", [2, CH], c1)
            gmv = sb("gmv", [NB, 2, 2], c1)
            gtm = sb("gtm", [NB, 2, 4], c1)
            raw = sb("raw", [768], c1)
            Wr = sb("Wr", [3, 2, 256], c1)
            grp = sb("grp", [128], c1)
            bst = sb("bst", [NB, 2, NCH, 6], c1)
            dma(grp[:, :], grp_d, [], "ldw")
            LDW = dma(Wr[:, :, :, :].rearrange("p m k n -> p (m k) n"),
                      wrkvo[0:3].rearrange("m (k p) n -> p (m k) n", p=128), [], "ldw")

            op("dve", lambda e: e.memset(xT[:, :, :, 0:1], 0.0), [], "cst")
            op("dve", lambda e: e.memset(mS[:, :, :, 0:1], LOW), [], "cst")
            op("dve", lambda e: e.memset(aS[:, :, :, 0:1], 0.0), [], "cst")
            op("dve", lambda e: e.memset(Bc[:, :, :], 0.0), [], "cst")
            CST = op("dve", lambda e: e.memset(bS[:, :, :, 0:1], LOW), [], "cst")

            M = {}

            def before(name, n, *rest):
                return M[(name, n, *rest)] if n >= 0 else None

            chunks = [(b, j) for j in range(NCH) for b in range(NB)]

            def load_x(n):
                b, j = chunks[n]
                p = n % 2
                M["ldx", n] = dma(xc[:, p, :, :], x[b, j * CH:(j + 1) * CH, :].rearrange("(w p) c -> p w c", p=128),
                                  [before("xtr", n - 2)], f"ldx{p}")

            def a_norm(n):
                p = n % 2
                for w in range(4):
                    s = op("dve", lambda e, w=w: e.bn_stats(mvs[:, w, 0:6], xc[:, p, w, :]), [M["ldx", n]], "a_st")
                    g = op("dve", lambda e, w=w: e.bn_aggr(mva[:, w, :], mvs[:, w, 0:6]), [s], "a_ag")
                r = op("dve", lambda e: e.tensor_scalar(rsd[:, :], mva[:, :, 1], EPS_LN, None, ALU.add),
                       [g], "a_rs")
                r = inv_sqrt(rsd[:, :], r, "a_rq")
                for w in range(4):
                    M["xn", n] = op("dve", lambda e, w=w: e.tensor_scalar(
                        xc[:, p, w, :], xc[:, p, w, :], mva[:, w, 0:1], rsd[:, w:w + 1], ALU.subtract, ALU.mult),
                        [r], "xn")

            def a_turn(n):
                b, j = chunks[n]
                p = n % 2
                for c in range(2):
                    for w in range(4):
                        M["xtr", n] = op("pe", lambda e, c=c, w=w: e.transpose(
                            PS[:, c, w * 128:(w + 1) * 128], xc[:, p, w, c * 128:(c + 1) * 128], ident[:, :]),
                            [M["xn", n], LD0, before("xT", n - 1)], "xtr" if (c, w) == (1, 3) else None)
                last = None
                if j:
                    last = op("act", lambda e: e.activation(xT[:, b, :, 0:1], xT[:, b, :, CH:CH + 1], ACT.Copy),
                              [M["mix", n - 2], M["xT", n - 2]], "xTc")
                M["xT", n] = op("act", lambda e: e.activation(xT[:, b, :, 1:CH + 1], PS[:, 0:2, :], ACT.Copy),
                                [M["xtr", n], last, CST], "xT")
                M["dx", n] = op("pool", lambda e: e.tensor_tensor(dx[:, :, :], xT[:, b, :, 1:CH + 1],
                                                                  xT[:, b, :, 0:CH], ALU.subtract),
                                [M["xT", n], before("rkv", n - 1, 2)], "dx")

            def mixed(i, c):
                return xm[:, i, c, :] if i < 2 else dx[:, c, :]

            def a_mix(n):
                b, j = chunks[n]
                for i, name in ((0, "mix_k"), (1, "mix_v"), (2, "mix_r")):
                    for c in range(2):
                        M["mix", n] = M["mix", n, i] = op("dve", lambda e, i=i, c=c, name=name: e.scalar_tensor_tensor(
                            out=mixed(i, c), in0=dx[:, c, :], scalar=V(name, c), in1=xT[:, b, c, 0:CH],
                            op0=ALU.mult, op1=ALU.add), [M["dx", n], before("rkv", n - 1, i)], "mix")

            def a_rkv(n):
                s = n % 3
                for i, wsel in ((0, 1), (1, 2), (2, 0)):
                    for g in range(2):
                        for c in range(2):
                            M["rkv", n, i] = op("pe", lambda e, i=i, g=g, c=c, wsel=wsel: e.matmul(
                                PS[:, 2 + 2 * i + g, :], Wr[:, wsel, c, g * 128:(g + 1) * 128], mixed(i, c),
                                start=(c == 0), stop=(c == 1)),
                                [M["mix", n, i], LDW, before("ev", n - 1, i)], f"rkv{i}" if (g, c) == (1, 1) else None)
                for i, dst, fn in ((0, kS, ACT.Copy), (1, vS, ACT.Copy), (2, sg, ACT.Sigmoid)):
                    M["ev", n, i] = op("act", lambda e, i=i, dst=dst, fn=fn: e.activation(
                        dst[:, s, :, :], PS[:, 2 + 2 * i:4 + 2 * i, :], fn),
                        [M["rkv", n, i], before("rw", n - 3)], f"ev{i}")

            def b_max(n):
                b, j = chunks[n]
                s = n % 3
                c = None
                if j:
                    c = op("dve", lambda e: e.tensor_copy(mS[:, b, :, 0:1], mS[:, b, :, CH:CH + 1]),
                           [M["msc", n - 2]], "msc0")
                for g in range(2):
                    M["msc", n] = op("dve", lambda e, g=g: e.tensor_tensor_scan(
                        mS[:, b, g, 1:CH + 1], wdec[:, g:g + 1].broadcast_to([128, CH]), kS[:, s, g, :],
                        mS[:, b, g, 0:1], ALU.add, ALU.max), [M["ev", n, 0], c, WU, CST, before("bS", n - 2)], "msc")
                for g in range(2):
                    M["q1", n] = op("dve", lambda e, g=g: e.scalar_tensor_tensor(
                        out=q1[:, g, :], in0=mS[:, b, g, 0:CH], scalar=wdec[:, g:g + 1], in1=mS[:, b, g, 1:CH + 1],
                        op0=ALU.add, op1=ALU.subtract), [M["msc", n]], "q1")
                M["km", n] = op("pool", lambda e: e.tensor_tensor(km[:, :, :], kS[:, s, :, :], mS[:, b, :, 1:CH + 1],
                                                                  ALU.subtract),
                                [M["msc", n], before("bsc", n - 1)], "km")
                M["ec", n] = op("act", lambda e: e.activation(q1[:, :, :], q1[:, :, :], ACT.Exp), [M["q1", n]], "ec")
                M["ed", n] = op("act", lambda e: e.activation(km[:, :, :], km[:, :, :], ACT.Exp), [M["km", n]], "ed")

            def b_sum(n):
                b, j = chunks[n]
                for g in range(2):
                    M["bsc", n] = op("dve", lambda e, g=g: e.tensor_tensor_scan(
                        BS[:, g, :], q1[:, g, :], km[:, g, :], Bc[:, b, g:g + 1], ALU.mult, ALU.add),
                        [M["ec", n], M["ed", n], before("Bc", n - 2), before("bS", n - 1), CST], "bsc")
                M["Bc", n] = op("dve", lambda e: e.tensor_copy(Bc[:, b, :], BS[:, :, CH - 1]), [M["bsc", n]], "Bc")
                M["lB", n] = op("act", lambda e: e.activation(BS[:, :, :], BS[:, :, :], ACT.Ln, bias=epsw[:, 0:1]),
                                [M["Bc", n], EPSM], "lB")
                c = None
                if j:
                    c = op("pool", lambda e: e.tensor_copy(bS[:, b, :, 0:1], bS[:, b, :, CH:CH + 1]),
                           [M["bS", n - 2], M["q2", n - 2]], "bSc")
                M["bS", n] = op("pool", lambda e: e.tensor_tensor(bS[:, b, :, 1:CH + 1], mS[:, b, :, 1:CH + 1],
                                                                  BS[:, :, :], ALU.add),
                                [M["lB", n], c, before("q2", n - 2), CST], "bS")

            def c_exps(n):
                b, j = chunks[n]
                s = n % 3
                for g in range(2):
                    M["q2", n] = op("dve", lambda e, g=g: e.scalar_tensor_tensor(
                        out=q2[:, g, :], in0=bS[:, b, g, 0:CH], scalar=wdec[:, g:g + 1], in1=kS[:, s, g, :],
                        op0=ALU.add, op1=ALU.subtract), [M["bS", n]], "q2")
                d = op("dve", lambda e: e.tensor_scalar(f[:, 0, :, :], q2[:, :, :], 0.0, None, ALU.min),
                       [M["q2", n]], "f0")
                x0 = op("act", lambda e: e.activation(f[:, 0, :, :], f[:, 0, :, :], ACT.Exp), [d], "x0")
                d = op("dve", lambda e: e.tensor_scalar(f[:, 1, :, :], q2[:, :, :], 0.0, None, ALU.max),
                       [M["q2", n]], "f1")
                x1 = op("act", lambda e: e.activation(f[:, 1, :, :], f[:, 1, :, :], ACT.Exp, scale=-1.0), [d], "x1")
                for g in range(2):
                    d = op("dve", lambda e, g=g: e.tensor_scalar(f[:, 3, g, :], q2[:, g, :], wu[:, g:g + 1], 0.0,
                                                                 ALU.subtract, ALU.max),
                           [M["q2", n], before("n2", n - 1)], "f3")
                x3 = op("act", lambda e: e.activation(f[:, 3, :, :], f[:, 3, :, :], ACT.Exp, scale=-1.0), [d], "x3")
                for g in range(2):
                    d = op("dve", lambda e, g=g: e.tensor_scalar(f[:, 2, g, :], q2[:, g, :], wu[:, g:g + 1], 0.0,
                                                                 ALU.subtract, ALU.min), [M["q2", n]], "f2")
                x2 = op("act", lambda e: e.activation(f[:, 2, :, :], f[:, 2, :, :], ACT.Exp), [d], "x2")
                M["x", n] = (x0, x1, x2, x3)
                M["evv", n] = op("pool", lambda e: e.tensor_tensor(f[:, 1, :, :], f[:, 1, :, :], vS[:, s, :, :],
                                                                   ALU.mult), [x1], "evv")
                M["n2", n] = op("pool", lambda e: e.tensor_tensor(n2[:, :, :], f[:, 3, :, :], vS[:, s, :, :],
                                                                  ALU.mult), [x3, before("num", n - 1)], "n2")

            def c_out(n):
                b, j = chunks[n]
                s, p = n % 3, n % 2
                x0, x1, x2, x3 = M["x", n]
                c = None
                if j:
                    c = op("dve", lambda e: e.tensor_copy(aS[:, b, :, 0:1], aS[:, b, :, CH:CH + 1]),
                           [M["asc", n - 2]], "asc0")
                for g in range(2):
                    M["asc", n] = op("dve", lambda e, g=g: e.tensor_tensor_scan(
                        aS[:, b, g, 1:CH + 1], f[:, 0, g, :], f[:, 1, g, :], aS[:, b, g, 0:1], ALU.mult, ALU.add),
                        [x0, M["evv", n], c, CST], "asc")
                n1 = op("dve", lambda e: e.tensor_tensor(q2[:, :, :], f[:, 2, :, :], aS[:, b, :, 0:CH], ALU.mult),
                        [x2, M["asc", n]], "n1")
                dn = op("dve", lambda e: e.scalar_tensor_tensor(
                    out=f[:, 2, :, :], in0=f[:, 2, :, :], scalar=epsw[:, 0:1], in1=f[:, 3, :, :],
                    op0=ALU.add, op1=ALU.add), [x3, EPSM], "dn")
                M["num", n] = op("dve", lambda e: e.tensor_tensor(q2[:, :, :], q2[:, :, :], n2[:, :, :], ALU.add),
                                 [n1, M["n2", n]], "num")
                ld = op("act", lambda e: e.activation(f[:, 2, :, :], f[:, 2, :, :], ACT.Ln), [dn], "ldn")
                rc = op("act", lambda e: e.activation(f[:, 2, :, :], f[:, 2, :, :], ACT.Exp, scale=-1.0), [ld], "rdn")
                ns = op("pool", lambda e: e.tensor_tensor(q2[:, :, :], q2[:, :, :], sg[:, s, :, :], ALU.mult),
                        [M["num", n], M["ev", n, 2]], "ns")
                M["rw", n] = op("dve", lambda e: e.tensor_tensor(rw[:, :, :], q2[:, :, :], f[:, 2, :, :], ALU.mult),
                                [ns, rc, before("str", n - 1)], "rw")
                for g in range(2):
                    M["bst", n] = op("dve", lambda e, g=g: e.bn_stats(bst[:, b, g, j, :], rw[:, g, :]),
                                     [M["rw", n]], "bst")
                M["str", n] = dma(rwkv_d[b, :, :, j * CH:(j + 1) * CH].rearrange("g p t -> p g t"), rw[:, :, :],
                                  [M["rw", n]], "str")

            def weight_pieces(l):
                w = w1[l].rearrange("(k p) n -> p k n", p=128)
                A, tl = slice(0, 128), slice(0, TAIL)
                ps = [(WQ, lambda t, k=k, o=o: t[:, k, o:o + 768], A, 768,
                       [(A, 0, 768, wqkv[l, k * 128:(k + 1) * 128, o:o + 768], 0)])
                      for k in range(2) for o in (0, 768)]
                ps += [(WO, lambda t, k=k: t[:, k:k + 2, :].rearrange("p k n -> p (k n)"), A, 512,
                        [(A, 0, 512, wo[l, k * 128:(k + 2) * 128, :].rearrange("(k p) n -> p k n", p=128), 2)])
                       for k in (0, 2)]
                for k in range(2):
                    ps.append((W1, lambda t, k=k: t[:, k, 0:640], A, 640, [(A, 0, 640, w[:, k, 0:640], 0)]))
                    ps.append((W1, lambda t, k=k: t[:, k, 640:1386], A, 746,
                               [(A, 0, 640, w[:, k, HID:HID + 640], 0), (A, 640, TAIL, w[:, k, 640:HID], 0),
                                (A, 704, TAIL, w[:, k, HID + 640:2 * HID], 0)]))
                ps += [(W2, lambda t, k=k, m=m: t[:, k:k + m, :].rearrange("p k n -> p (k n)"), A, m * 256,
                        [(A, 0, m * 256, w2[l, k * 128:(k + m) * 128, :].rearrange("(k p) n -> p k n", p=128), m)])
                       for k, m in ((0, 3), (3, 2))]
                ps.append((W2, lambda t: t[0:TAIL + 1, 5, :], slice(0, TAIL + 1), 256,
                           [(tl, 0, 256, w2[l, 640:HID, :], 0), (slice(TAIL, TAIL + 1), 0, 256, b2[l:l + 1, :], 0)]))
                return ps

            split = [None]

            def split_piece(piece, waits):
                tiles, view, rows, n, parts = piece
                ws = [split[0]] + waits
                zero = None
                if n == 746:
                    zero = op("pool", lambda e: e.memset(raw[:, 640 + TAIL:704], 0.0), ws, "w_z")
                for r, c, w, src, k in parts:
                    dst = raw[r, c:c + w]
                    m = dma(dst.rearrange("p (k n) -> p k n", k=k) if k else dst, src, ws, "w_ld")
                h = op("act", lambda e: e.activation(view(tiles[0]), raw[rows, 0:n], ACT.Copy), [m, zero] + waits, "w_hi")
                split[0] = op("pool", lambda e: e.tensor_tensor(view(tiles[1]), raw[rows, 0:n],
                                                                view(tiles[0]).bitcast(F32), ALU.subtract),
                              [h, m, zero] + waits, "w_lo")

            def store_layer():
                for a in (0, 1):
                    for d, t in ((wq_d, WQ), (wo_d, WO), (w1_d, W1)):
                        dma(d[a], t[a][:, :, :].bitcast(F32), [split[0]], "w_st")
                    dma(w2_d[a][:, 0:5, :], W2[a][:, 0:5, :].bitcast(F32), [split[0]], "w_st")
                    m = dma(w2_d[a][0:TAIL + 1, 5, :], W2[a][0:TAIL + 1, 5, :].bitcast(F32), [split[0]], "w_st")
                return m

            N = len(chunks)
            load_x(0)
            load_x(1)
            todo = [(l, p) for l in (1, 0) for p in weight_pieces(l)]
            WST = None
            for i in range(N + 2):
                if i < N:
                    a_norm(i)
                    a_turn(i)
                    if i + 2 < N:
                        load_x(i + 2)
                if 1 <= i <= N:
                    b_max(i - 1)
                if i >= 2:
                    c_exps(i - 2)
                if i < N:
                    a_mix(i)
                    a_rkv(i)
                if 1 <= i <= N:
                    b_sum(i - 1)
                if i >= 2:
                    c_out(i - 2)
                for l, piece in todo[2 * i:2 * i + 2]:
                    if l == 0 and WST is None:
                        WST = store_layer()
                    split_piece(piece, [WST] if WST else [])
            SPLIT_DONE = [split[0], WST]

            for b in range(NB):
                for g in range(2):
                    m = op("dve", lambda e, b=b, g=g: e.bn_aggr(
                        gmv[:, b, g, :], bst[:, b, g, :, :].rearrange("p j s -> p (j s)")), [M["bst", N - 1]], "gag")
            G1 = op("pe", lambda e: e.matmul(PS[:, 0, 0:4], grp[:, :], gmv[:, :, :, 0].rearrange("p b g -> p (b g)"),
                                             start=True, stop=True), [m, M["xT", N - 1], LDW], "g1")
            m = op("dve", lambda e: e.tensor_copy(gtm[:, :, :, 0], PS[:, 0, 0:4].rearrange("p (b g) -> p b g", b=2)),
                   [G1], "g2")
            m = op("dve", lambda e: e.tensor_tensor(gtm[:, :, :, 1], gmv[:, :, :, 0], gtm[:, :, :, 0], ALU.subtract),
                   [m], "g2")
            m = op("dve", lambda e: e.tensor_tensor(gtm[:, :, :, 2], gtm[:, :, :, 1], gtm[:, :, :, 1], ALU.mult),
                   [m], "g2")
            m = op("dve", lambda e: e.tensor_tensor(gtm[:, :, :, 3], gtm[:, :, :, 2], gmv[:, :, :, 1], ALU.add),
                   [m], "g2")
            G3 = op("pe", lambda e: e.matmul(PS[:, 1, 0:4], grp[:, :], gtm[:, :, :, 3].rearrange("p b g -> p (b g)"),
                                             start=True, stop=True), [m], "g1")
            m = op("dve", lambda e: e.tensor_scalar(gsc[:, :, :], PS[:, 1, 0:4].rearrange("p (b g) -> p b g", b=2),
                                                    EPS_LN, None, ALU.add), [G3], "g2")
            m = inv_sqrt(gsc[:, :, :].rearrange("p b g -> p (b g)"), m, "g4")
            for b in range(NB):
                m2 = op("dve", lambda e, b=b: e.tensor_tensor(gsc[:, b, :], gsc[:, b, :],
                                                              vecs[:, VEC["gamma"]:VEC["gamma"] + 2], ALU.mult),
                        [m], "g2")
            m = op("dve", lambda e: e.tensor_tensor(gtm[:, :, :, 1], gtm[:, :, :, 0], gsc[:, :, :], ALU.mult),
                   [m2], "g2")
            for b in range(NB):
                GN = op("dve", lambda e, b=b: e.tensor_tensor(gsh[:, b, :], vecs[:, VEC["beta"]:VEC["beta"] + 2],
                                                              gtm[:, b, :, 1], ALU.subtract), [m], "g2")
            STORED = [M["str", N - 1]]

        U = 2 * NG
        NY, NV, NX = 10, 5, 7
        mask = sb("mask", [2, 256])
        qsks = sb("qsks", [2, 256])
        xin = sb("xin", [2, 256])
        rk = sb("rk", [2, 2, 128])
        nT = sb("nT", [2, 128])
        x1 = sb("x1", [2, 256])
        x1i = sb("x1i", [2, 256])
        st0 = sb("st0", [6])
        mv0 = sb("mv0", [2])
        r0 = sb("r0", [1])
        y = sb("y", [NY, 256])
        tb = sb("tb", [2, 256])
        rt = sb("rt", [2, 256])
        hT = pair("hT", [2, 129])
        sq = sb("sq", [1024])
        ss = sb("ss", [16])
        rs = sb("rs", [2, 16])
        sc = sb("sc", [4, 8])
        Ar = sb("Ar", [1024])
        Br = sb("Br", [1024])
        qT = pair("qT", [4, 128])
        kT = pair("kT", [2, 4, 128])
        vv = sb("vv", [NV, 8, 2, 64], dt=F32R)
        Sm = sb("Sm", [8, 256])
        mx = sb("mx", [8])
        sm = sb("sm", [2, 8])
        oU = sb("oU", [2, 4, 64])
        nb = sb("nb", [8])
        PT = pair("PT", [8, 256])
        ro = sb("ro", [8])
        oS = sb("oS", [8, 64])
        oT = pair("oT", [4, 128])
        x2 = sb("x2", [NX, 256])
        h2 = sb("h2", [3, 128])
        st1 = sb("st1", [12])
        mv1 = sb("mv1", [2, 2])
        r1 = sb("r1", [2, 1])
        z = sb("z", [2, 256])
        zf = sb("zf", [2, 128])
        zT = pair("zT", [2, 256])
        Gl = sb("Gl", [4, 256])
        uT = pair("uT", [6, 256])
        os_ = sb("os", [2, 256])

        first = [GN] + STORED + SPLIT_DONE
        op("dve", lambda e: e.memset(uT[0][0:64, 5, :].bitcast(F32), 1.0), first, "end")
        op("dve", lambda e: e.memset(h2[0:1, :, :], 0.0), [], "end")
        END = op("dve", lambda e: e.memset(uT[1][0:64, 5, :].bitcast(F32), 0.0), [], "end")
        for eng in ("pe", "act", "pool", "sp"):
            op(eng, None, [END])
        dma(mask[:, :, :], mask_d, [END], "ld2")
        LD2 = dma(qsks[:, :, :], qsk, [END], "ld2")

        M = {}

        def before(name, n, *rest):
            return M[(name, n, *rest)] if n >= 0 else None

        def first_win(n):
            return n % NWIN == 0

        def place(n):
            l, g = divmod(n, NG)
            return l, g, g // NWIN, g % NWIN

        held = [[M0] for M0 in [END] * 8]
        turn = [0]

        def bank():
            b = turn[0] % 8
            turn[0] += 1
            free, held[b] = held[b], None
            return b, free + []

        def mm3(dst, L, R, start, stop, waits, sig):
            prods = ((0, 0), (1, 0), (0, 1))
            for i, (a, b) in enumerate(prods):
                last = op("pe", lambda e, a=a, b=b, i=i: e.matmul(dst, L(a), R(b), start=start and i == 0,
                                                                  stop=stop and i == 2),
                          waits, sig if i == 2 else None)
            return last

        def high(dst, src, waits, sig):
            return op("act", lambda e: e.activation(dst, src, ACT.Copy), waits, sig)

        def low(dst, src, hi, waits, sig, eng="dve"):
            return op(eng, lambda e: e.tensor_tensor(dst, src, hi.bitcast(F32), ALU.subtract), waits, sig)

        WREADY = {}

        def loads(n):
            l, g, b, w = place(n)
            rows = slice(w * 128, (w + 1) * 128)
            if l == 0:
                M["lrk", n] = dma(rk[:, n % 2, :, :], rwkv_d[b, :, :, rows].rearrange("g p t -> p g t"),
                                  [before("nT", n - 2)] + STORED, f"lrk{n % 2}")

        def load_x(n):
            l, g, b, w = place(n)
            if l == 0:
                M["lxi", n] = dma(xin[:, n % 2, :], x[b, w * 128:(w + 1) * 128, :], [before("x1", n - 2)],
                                  f"lxi{n % 2}")

        def load_y(n):
            l, g, b, w = place(n)
            rows = slice(w * 128, (w + 1) * 128)
            if l:
                M["y", n] = dma(y[:, n % NY, :], y_d[b, rows, :], [M["x2", n - NY], M["sty", g]], f"ly{n % 4}")

        def load_tab(n):
            l, g, b, w = place(n)
            rows = slice(w * 128, (w + 1) * 128)
            M["ltb", n] = dma(tb[:, n % 2, :], tab[rows, :], [before("rt", n - 2)], f"ltb{n % 2}")

        def load_x1(n):
            l, g, b, w = place(n)
            if l:
                M["lx1", n] = dma(x1i[:, n % 2, :], x1_d[b, w * 128:(w + 1) * 128, :],
                                  [M["stx", g], M["os", n - 2] if g >= 2 else None], f"lx1{n % 2}")

        def pre_norm(n):
            l, g, b, w = place(n)
            if l:
                return
            for c in range(2):
                M["nT", n] = op("pool", lambda e, c=c: e.tensor_scalar(
                    nT[:, c, :], rk[:, n % 2, c, :], gsc[:, b, c:c + 1], gsh[:, b, c:c + 1], ALU.mult, ALU.add),
                    [M["lrk", n], before("p0", n - 1), GN], "nT")

        def pre_mm(n):
            l, g, b, w = place(n)
            if l:
                return
            k, free = bank()
            for c in range(2):
                M["p0", n] = op("pe", lambda e, c=c: e.matmul(PS[:, k, 0:256], nT[:, c, :], Wp[:, c, :],
                                                              start=(c == 0), stop=(c == 1)),
                                [M["nT", n]] + free, "p0" if c else None)
            a = M["x1", n] = op("dve", lambda e: e.tensor_tensor(x1[:, n % 2, :], PS[:, k, 0:256], xin[:, n % 2, :],
                                                                 ALU.add),
                                [M["p0", n], M["lxi", n], before("y0", n - 2), before("stx", n - 2)], "x1")
            held[k] = [a]
            M["stx", n] = dma(x1_d[b, w * 128:(w + 1) * 128, :], x1[:, n % 2, :], [a], f"stx{n % 2}")
            a = op("dve", lambda e: e.bn_stats(st0[:, 0:6], x1[:, n % 2, :]), [a], "ps")
            a = op("dve", lambda e: e.bn_aggr(mv0[:, :], st0[:, 0:6]), [a, before("y0", n - 1)], "ps")
            a = op("dve", lambda e: e.tensor_scalar(r0[:, :], mv0[:, 1:2], EPS_LN, None, ALU.add), [a], "ps")
            M["r0", n] = inv_sqrt(r0[:, :], a, "r0")

        def pre_y(n):
            if n < NG:
                M["y", n] = M["y0", n] = op("dve", lambda e: e.tensor_scalar(
                    y[:, n % NY, :], x1[:, n % 2, :], mv0[:, 0:1], r0[:, 0:1], ALU.subtract, ALU.mult),
                    [M["r0", n], before("x2", n - NY)], "y0")

        def a_rt(n):
            l = n // NG
            M["rt", n] = op("pool", lambda e: e.tensor_tensor(rt[:, n % 2, :], tb[:, n % 2, :], qsks[:, l, :],
                                                              ALU.mult),
                            [M["ltb", n], LD2, before("rope", n - 2, 0)], "rt")

        def a_hT(n):
            k, free = bank()
            for c in range(2):
                t = op("pe", lambda e, c=c: e.transpose(PS[:, k, c * 128:(c + 1) * 128],
                                                        y[:, n % NY, c * 128:(c + 1) * 128], ident[:, :]),
                       [M["y", n]] + free, "p1" if c else None)
            used = before("p2", n - 1, 2)
            if first_win(n):
                c0 = [op("dve", lambda e, a=a: e.memset(hT[a][:, 1, 0:1].bitcast(F32), 0.0), [used], "hTc") for a in (0, 1)]
            else:
                c0 = [op("act", lambda e: e.activation(hT[0][:, 1, 0:1], hT[0][:, 1, 128:129].bitcast(F32), ACT.Copy),
                         [used, M["hTh", n - 1]], "hTa"),
                      op("dve", lambda e: e.tensor_copy(hT[1][:, 1, 0:1], hT[1][:, 1, 128:129].bitcast(F32)),
                         [used, M["hT", n - 1][-1]], "hTc")]
            src = PS[:, k, 0:256].rearrange("p (c t) -> p c t", c=2)
            h = M["hTh", n] = high(hT[0][:, :, 1:129], src, [t, used] + c0, "hTh")
            lo = low(hT[1][:, :, 1:129], src, hT[0][:, :, 1:129], [h] + c0, "hTl")
            held[k] = [lo]
            M["hT", n] = c0 + [h, lo]

        def a_qkv(n, i):
            l = n // NG
            k, free = bank()
            M["qb", n, i] = k
            for c in range(2):
                M["p2", n, i] = mm3(PS[:, k, :], lambda a, c=c: hT[a][:, c, 1 - c:129 - c],
                                    lambda a, c=c: WQ[a][:, c, i * 512:(i + 1) * 512], c == 0, c == 1,
                                    M["hT", n] + free + [WREADY.get(("q", l))], "p2" if c else None)

        def a_square(n, i):
            k = M["qb", n, i]
            M["sq", n, i] = op("act", lambda e: e.activation(sq[:, i * 512:(i + 1) * 512], PS[:, k, :], ACT.Square),
                               [M["p2", n, i], before("ss", n - 1)], "sq")

        def a_rope(n, i):
            k = M["qb", n, i]
            X = PS[:, k, :].rearrange("p (h d) -> p h d", h=8)
            A = Ar[:, i * 512:(i + 1) * 512].rearrange("p (h d) -> p h d", h=8)
            B = Br[:, i * 512:(i + 1) * 512].rearrange("p (h d) -> p h d", h=8)
            t0 = rt[:, n % 2, i * 128:i * 128 + 64].unsqueeze(1)
            t1 = rt[:, n % 2, i * 128 + 64:i * 128 + 128].unsqueeze(1)
            ws = [M["sq", n, i], M["rt", n], before("p3", n - 1, i), before("kr" if i else "qr", n - 1)]
            op("dve", lambda e: e.tensor_tensor(A, X, t0.broadcast_to([128, 8, 64]), ALU.mult), ws)
            op("dve", lambda e: e.tensor_tensor(B[:, :, 0:32], X[:, :, 32:64],
                                                t1[:, :, 0:32].broadcast_to([128, 8, 32]), ALU.mult), ws)
            M["rope", n, i] = op("dve", lambda e: e.tensor_tensor(
                B[:, :, 32:64], X[:, :, 0:32], t1[:, :, 32:64].broadcast_to([128, 8, 32]), ALU.mult), ws, "rope")
            held[k] = [M["rope", n, i]]

        def a_v(n):
            k = M["qb", n, 2]
            src = PS[:, k, :].rearrange("p (h d) -> p h d", h=8)
            s = n % NV
            used = before("p6", n - NV + 1, 1)
            h = high(vv[:, s, :, 0, :], src, [M["p2", n, 2], used], "vh")
            M["v", n] = low(vv[:, s, :, 1, :], src, vv[:, s, :, 0, :], [h, used], "vl")
            held[k] = [M["v", n]]

        def a_sums(n):
            M["ss", n] = op("dve", lambda e: e.tensor_reduce(
                ss[:, :], sq[:, :].rearrange("p (h d) -> p h d", h=16), AX_X, ALU.add),
                [M["sq", n, 0], M["sq", n, 1]], "ss")
            M["rsm", n] = op("dve", lambda e: e.tensor_scalar(rs[:, n % 2, :], ss[:, :], 1e-24, None, ALU.max),
                             [M["ss", n], before("kn", n - 2), before("sc", n - 2)], "rsm")

        def a_rot(n):
            for i, name in ((1, "kr"), (0, "qr")):
                r = slice(i * 512, (i + 1) * 512)
                M[name, n] = op("pool", lambda e, r=r: e.tensor_tensor(Ar[:, r], Ar[:, r], Br[:, r], ALU.add),
                                [M["rope", n, i]], name)

        def a_scale(n):
            M["rs", n] = inv_sqrt(rs[:, n % 2, :], M["rsm", n], "rs")
            A = Ar[:, 512:1024].rearrange("p (h d) -> p h d", h=8)
            M["kn", n] = op("pool", lambda e: e.tensor_tensor(
                A, A, rs[:, n % 2, 8:16].unsqueeze(2).broadcast_to([128, 8, 64]), ALU.mult),
                [M["kr", n], M["rs", n]], "kn")
            M["sc", n] = op("pool", lambda e: e.tensor_scalar(sc[:, n % 4, :], rs[:, n % 2, 0:8], 8.0, None, ALU.mult),
                            [M["rs", n], before("ex", n - 4, 1)], "sc")

        def a_qkT(n, i):
            k, free = bank()
            for c in range(4):
                M["p3", n, i] = op("pe", lambda e, c=c: e.transpose(
                    PS[:, k, c * 128:(c + 1) * 128], Ar[:, i * 512 + c * 128:i * 512 + (c + 1) * 128], ident[:, :]),
                    [M["kn" if i else "qr", n]] + free, "p3" if c == 3 else None)
            used = before("p4", n - 1, 1)
            d = [(kT[a][:, n % 2, :, :] if i else qT[a][:, :, :]).rearrange("p c t -> p (c t)") for a in (0, 1)]
            h = high(d[0], PS[:, k, :], [M["p3", n, i], used], "qkh")
            lo = low(d[1], PS[:, k, :], d[0], [h, used], "qkl")
            held[k] = [lo]
            M["qkT", n, i] = lo

        def cols(n):
            return (n % 2 * 128, n % 2 * 128 + 128) if first_win(n) else (0, 256)

        def b_scores(n, q):
            c0, c1 = cols(n)
            ks = [bank(), bank()]
            for h in range(4 * q, 4 * q + 4):
                p0 = 64 * (h % 2)
                k, free = ks[h % 2]
                dst = PS[:, k, (h // 2 % 2) * 256 + c0:(h // 2 % 2) * 256 + c1]

                def R(a, p0=p0, h=h):
                    return kT[a][p0:p0 + 64, n % 2, h // 2, :] if first_win(n) else kT[a][p0:p0 + 64, :, h // 2, :]

                M["p4", n, q] = M["p4", n, q, h % 2] = mm3(
                    dst, lambda a, p0=p0, h=h: qT[a][p0:p0 + 64, h // 2, :], R, True, True,
                    [M["qkT", n, 0], M["qkT", n, 1]] + free, "p4" if h % 4 >= 2 else None)
            for h in (4 * q, 4 * q + 2, 4 * q + 1, 4 * q + 3):
                k = ks[h % 2][0]
                m = op("dve", lambda e, h=h, k=k: e.tensor_tensor_reduce(
                    Sm[:, h, c0:c1], PS[:, k, (h // 2 % 2) * 256 + c0:(h // 2 % 2) * 256 + c1],
                    mask[:, n % 2, c0:c1], 1.0, -3.0e38, ALU.add, ALU.max, mx[:, h:h + 1]),
                    [M["p4", n, q, h % 2], before("p5", n - 1, h // 2), LD2], "mx")
                held[k] = [m]
            M["mx", n, q] = m
            r = slice(4 * q, 4 * q + 4)
            M["nb", n, q] = op("dve", lambda e: e.scalar_tensor_tensor(
                out=nb[:, r], in0=mx[:, r], scalar=-1.0, in1=sc[:, n % 4, r], op0=ALU.mult, op1=ALU.mult),
                [m, M["sc", n], before("ex", n - 1, q)], "nb")

        def b_exp(n, q):
            c0, c1 = cols(n)
            for h in range(4 * q, 4 * q + 4):
                M["ex", n, q] = M["exh", n, h] = op("act", lambda e, h=h: e.activation(
                    Sm[:, h, c0:c1], Sm[:, h, c0:c1], ACT.Exp, bias=nb[:, h:h + 1], scale=sc[:, n % 4, h:h + 1],
                    accum_out=sm[:, n % 2, h:h + 1]), [M["nb", n, q], before("ro", n - 2, q)], "ex")

        def b_turn(n, j):
            c0, c1 = cols(n)
            k, free = bank()
            for i in range(2):
                for c in range(c0, c1, 128):
                    M["p5", n, j] = op("pe", lambda e, i=i, c=c: e.transpose(
                        PS[:, k, i * 256 + c:i * 256 + c + 128], Sm[:, 2 * j + i, c:c + 128], ident[:, :]),
                        [M["exh", n, 2 * j + 1]] + free, "p5" if i and c + 128 == c1 else None)
            used = before("p6", n - 1, j // 2)
            src = PS[:, k, :].rearrange("p (h j) -> p h j", h=2)[:, :, c0:c1]
            d = [PT[a][:, 2 * j:2 * j + 2, c0:c1] for a in (0, 1)]
            h = high(d[0], src, [M["p5", n, j], used], "pth")
            M["PT", n, j] = low(d[1], src, d[0], [h, used], "ptl")
            held[k] = [M["PT", n, j]]

        def b_pv(n, q):
            sides = [n % 2] if first_win(n) else [1 - n % 2, n % 2]
            k, free = bank()
            ws = [M["PT", n, 2 * q], M["PT", n, 2 * q + 1], M["v", n]] + free
            for i in range(4):
                h = 4 * q + i
                for s in sides:
                    v = n % NV if s == n % 2 else (n - 1) % NV
                    P = [PT[a][:, h, s * 128:(s + 1) * 128] for a in (0, 1)]
                    op("pe", lambda e, i=i, h=h, s=s, v=v, P=P: e.matmul(
                        PS[:, k, 128 * i:128 * i + 128], P[0], vv[:, v, h, :, :].rearrange("p a d -> p (a d)"),
                        start=s == sides[0], stop=False), ws)
                    M["p6", n, q] = op("pe", lambda e, i=i, h=h, s=s, v=v, P=P: e.matmul(
                        PS[:, k, 128 * i:128 * i + 64], P[1], vv[:, v, h, 0, :], start=False, stop=s == sides[-1]),
                        ws, "p6" if i == 3 and s == sides[-1] else None)
            O = PS[:, k, :].rearrange("p (h d) -> p h d", h=4)
            r = slice(4 * q, 4 * q + 4)
            M["ro", n, q] = op("dve", lambda e: e.reciprocal(ro[:, r], sm[:, n % 2, r]),
                               [M["ex", n, q], before("on", n - 1, q)], "ro")
            rb = ro[:, r].unsqueeze(2).broadcast_to([128, 4, 64])
            a = op("dve", lambda e: e.tensor_tensor(oU[:, q, :, :], O[:, :, 64:128], rb, ALU.mult),
                   [M["p6", n, q], M["ro", n, q], before("on", n - 1, q)], "ou")
            b = op("dve", lambda e: e.tensor_tensor(oS[:, r, :], O[:, :, 0:64], rb, ALU.mult),
                   [M["p6", n, q], M["ro", n, q], before("p7", n - 1)], "ou")
            M["on", n, q] = op("pool", lambda e: e.tensor_tensor(oS[:, r, :], oS[:, r, :], oU[:, q, :, :], ALU.add),
                               [a, b], "on")
            held[k] = [b]

        def c_oT(n):
            k, free = bank()
            for c in range(4):
                M["p7", n] = op("pe", lambda e, c=c: e.transpose(
                    PS[:, k, c * 128:(c + 1) * 128], oS[:, 2 * c:2 * c + 2, :].rearrange("p h d -> p (h d)"),
                    ident[:, :]), [M["on", n, 0], M["on", n, 1]] + free, "p7" if c == 3 else None)
            d = [oT[a][:, :, :].rearrange("p c t -> p (c t)") for a in (0, 1)]
            h = high(d[0], PS[:, k, :], [M["p7", n], before("p8", n - 1)], "oTh")
            M["oT", n] = low(d[1], PS[:, k, :], d[0], [h, before("p8", n - 1)], "oTl")
            held[k] = [M["oT", n]]

        def c_wo(n):
            l = n // NG
            k, free = bank()
            for c in range(4):
                M["p8", n] = mm3(PS[:, k, 0:256], lambda a, c=c: oT[a][:, c, :], lambda a, c=c: WO[a][:, c, :],
                                 c == 0, c == 3, [M["oT", n], WREADY.get(("o", l))] + free, "p8" if c == 3 else None)
            M["x2", n] = op("dve", lambda e: e.tensor_tensor(x2[:, n % NX, :], PS[:, k, 0:256], y[:, n % NY, :],
                                                             ALU.add),
                            [M["p8", n], M["y", n], before("x3", n - NX), before("h2", n - NX + 1)], "x2")
            held[k] = [M["x2", n]]

        def c_shift(n):
            s = n % 3
            ws = [M["x2", n], before("z", n - 3)]
            if first_win(n):
                if n:
                    ws.append(op("dve", lambda e: e.memset(h2[0:1, s, :], 0.0), [before("z", n - 3)], "h2z"))
            else:
                dma(h2[0:1, s, :], x2[127:128, (n - 1) % NX, 128:256], ws, f"h2{s}")
            M["h2", n] = dma(h2[1:128, s, :], x2[0:127, n % NX, 128:256], ws, f"h2{s}")

        def c_stats(n):
            a0 = op("dve", lambda e: e.bn_stats(st1[:, 0:6], x2[:, n % NX, 0:128]), [M["x2", n]], "ls")
            a = op("dve", lambda e: e.bn_stats(st1[:, 6:12], h2[:, n % 3, :]), [M["h2", n]], "ls")
            a = op("dve", lambda e: e.bn_aggr(mv1[:, n % 2, :], st1[:, :]), [a0, a, before("z", n - 2)], "ls")
            a = op("dve", lambda e: e.tensor_scalar(r1[:, n % 2, :], mv1[:, n % 2, 1:2], EPS_LN, None, ALU.add), [a], "ls")
            M["r1", n] = inv_sqrt(r1[:, n % 2, :], a, "r1")

        def c_z(n):
            used = before("p10", n - 2)
            op("dve", lambda e: e.tensor_scalar(z[:, n % 2, 0:128], x2[:, n % NX, 0:128], mv1[:, n % 2, 0:1], r1[:, n % 2, 0:1],
                                                ALU.subtract, ALU.mult), [M["r1", n], M["h2", n], used])
            M["z", n] = op("dve", lambda e: e.tensor_scalar(z[:, n % 2, 128:256], h2[:, n % 3, :], mv1[:, n % 2, 0:1], r1[:, n % 2, 0:1],
                                                            ALU.subtract, ALU.mult), [M["r1", n], used], "z")

        def c_zT(n):
            l = n // NG
            k, free = bank()
            for c in range(2):
                M["p10", n] = op("pe", lambda e, c=c: e.transpose(PS[:, k, c * 128:(c + 1) * 128],
                                                                  z[:, n % 2, c * 128:(c + 1) * 128], ident[:, :]),
                                 [M["z", n]] + free, "p10" if c else None)
            for c in range(2):
                m = op("act", lambda e, c=c: e.activation(
                    zf[:, c, :], PS[:, k, c * 128:(c + 1) * 128], ACT.Identity, bias=V("lb", 2 * l + c),
                    scale=V("lg", 2 * l + c)), [M["p10", n], before("zT", n - 1)], "zf")
            held[k] = [m]
            used = before("p11", n // 2 - 1, 2)
            half = slice(n % 2 * 128, n % 2 * 128 + 128)
            h = high(zT[0][:, :, half], zf[:, :, :], [m, used], "zTh")
            M["zT", n] = low(zT[1][:, :, half], zf[:, :, :], zT[0][:, :, half], [h, used], "zTl", "pool")

        def c_mlp(m, part):
            l = 2 * m // NG
            kg, fg = bank()
            ka, fa = bank()
            if part < 2:
                j0 = 2 * part
                prods = [(kg, fg, i, 640 + (j0 + i) * 128, 128) for i in (0, 1)] + \
                        [(ka, fa, i, (j0 + i) * 128, 128) for i in (0, 1)]
                glus = [j0, j0 + 1]
            else:
                prods = [(kg, fg, 0, 640 + 512, 128), (kg, fg, 1, 1280, 106), (ka, fa, 0, 512, 128)]
                glus = [4, 5]
            for k, free, o, wcol, w in prods:
                for c in range(2):
                    done = mm3(PS[0:w, k, o * 256:o * 256 + 256],
                               lambda a, c=c, wcol=wcol, w=w: W1[a][:, c, wcol:wcol + w], lambda a, c=c: zT[a][:, c, :],
                               c == 0, c == 1, [M["zT", 2 * m], M["zT", 2 * m + 1], WREADY.get(("1", l))] + free,
                               "p11" if c else None)
                M["p11", m, part] = done
                if k == kg:
                    gdone = done
            for j in glus:
                lo, hi = (64, 64 + TAIL) if j == 5 else (0, 128)
                o = j % 2 * 256
                bi = vecs[lo:hi, VEC["b1g"] + 6 * l + j:VEC["b1g"] + 6 * l + j + 1]
                M["gl", m, j] = op("act", lambda e, lo=lo, hi=hi, o=o, bi=bi, j=j: e.activation(
                    Gl[lo:hi, j % 4, :], PS[lo:hi, kg, o:o + 256], ACT.Gelu, bias=bi),
                    [gdone, M["u", m, 0] if part == 2 else before("u", m - 1, 2 - part)], "gl")
            for j in glus:
                if j == 5:
                    s, w, gl = PS[0:TAIL, kg, 256:512], TAIL, Gl[64:64 + TAIL, 1, :]
                else:
                    s, w, gl = PS[:, ka, j % 2 * 256:j % 2 * 256 + 256], 128, Gl[:, j % 4, :]
                bi = vecs[0:w, VEC["b1a"] + 6 * l + j:VEC["b1a"] + 6 * l + j + 1]
                M["glu", m, part] = op("dve", lambda e, s=s, w=w, gl=gl, bi=bi, j=j: e.scalar_tensor_tensor(
                    out=Gl[0:w, j % 4, :], in0=s, scalar=bi, in1=gl, op0=ALU.add, op1=ALU.mult),
                    [M["p11", m, part], M["gl", m, j]], "glu")
            held[kg] = [M["glu", m, part], M["gl", m, glus[-1]]]
            held[ka] = [M["glu", m, part]]

        def c_u(m, part):
            used = before("p12", 2 * m - 1)
            A = slice(0, 128)
            for r, j, g in (((A, slice(2 * part, 2 * part + 2), slice(2 * part, 2 * part + 2)),) if part < 2 else
                            ((A, slice(4, 5), slice(0, 1)), (slice(0, TAIL), slice(5, 6), slice(1, 2)))):
                h = high(uT[0][r, j, :], Gl[r, g, :], [M["glu", m, part], used], "uh")
                M["u", m, part] = low(uT[1][r, j, :], Gl[r, g, :], uT[0][r, j, :], [h, used], "ul", "pool")

        def c_w2(n):
            l, g, b, w = place(n)
            k, free = bank()
            for j in range(6):
                kk = 128 if j < 5 else TAIL + 1
                M["p12", n] = mm3(PS[:, k, 0:256], lambda a, j=j, kk=kk: uT[a][0:kk, j, n % 2 * 128:n % 2 * 128 + 128],
                                  lambda a, j=j, kk=kk: W2[a][0:kk, j, :], j == 0, j == 5,
                                  [M["u", n // 2, 0], M["u", n // 2, 1], M["u", n // 2, 2], WREADY.get(("2", l))] + free, "p12" if j == 5 else None)
            a = M["x3", n] = op("dve", lambda e: e.tensor_tensor(os_[:, n % 2, :], PS[:, k, 0:256], x2[:, n % NX, :],
                                                                 ALU.add),
                                [M["p12", n], before("sto", n - 2)], "x3")
            held[k] = [a]
            rows = slice(w * 128, (w + 1) * 128)
            if l == 0:
                M["sto", n] = M["sty", g] = dma(y_d[b, rows, :], os_[:, n % 2, :], [a], f"sto{n % 2}")
                return
            a = M["os", n] = op("pool", lambda e: e.tensor_tensor(os_[:, n % 2, :], os_[:, n % 2, :],
                                                                  x1i[:, n % 2, :], ALU.add),
                                [a, M["lx1", n]], "os")
            M["sto", n] = dma(out[b, rows, :], os_[:, n % 2, :], [a], f"sto{n % 2}")

        def reload(key, pairs, last):
            for dst, src in pairs:
                WREADY[key, 1] = dma(dst.bitcast(F32), src, [last, SPLIT_DONE[-1]], "w_re" + key)

        RELOAD = {
            4: lambda n: reload("q", [(WQ[a][:, :, :], wq_d[a]) for a in (0, 1)], M["p2", n, 2]),
            10: lambda n: reload("o", [(WO[a][:, :, :], wo_d[a]) for a in (0, 1)], M["p8", n]),
            14: lambda n: reload("1", [(W1[a][:, :, :], w1_d[a]) for a in (0, 1)], M["p11", n // 2, 2]),
            15: lambda n: reload("2", [(W2[a][r, j, :], w2_d[a][r, j, :]) for a in (0, 1)
                                       for r, j in ((slice(0, 128), slice(0, 5)), (slice(0, TAIL + 1), slice(5, 6)))],
                                 M["p12", n]),
        }

        def pairs(stage, which):
            return lambda n, *rest: stage(n // 2 if which is None else n - 1 + which, *rest) if n % 2 else None

        def parity(stage, odd):
            return lambda n, *rest: stage(n, *rest) if n % 2 == odd else None

        ORDER = [
            (12, c_z), (11, c_stats), (5, a_scale),
            (13, parity(c_zT, 1)), (10, c_wo), (10, c_shift), (9, c_oT), (8, b_pv, 0),
            (14, pairs(c_mlp, None), 0), (14, pairs(c_u, None), 0), (15, pairs(c_w2, 0)),
            (7, b_turn, 0), (7, b_turn, 1), (8, b_pv, 1),
            (14, pairs(c_mlp, None), 1), (14, pairs(c_u, None), 1), (15, pairs(c_w2, 1)),
            (7, b_turn, 2), (7, b_turn, 3), (14, pairs(c_mlp, None), 2), (14, pairs(c_u, None), 2),
            (6, b_scores, 0), (4, a_qkv, 1), (4, a_square, 1), (6, b_scores, 1),
            (5, a_qkT, 1), (4, a_rope, 1), (4, a_qkv, 0), (4, a_square, 0), (5, a_qkT, 0), (4, a_rope, 0),
            (4, a_qkv, 2), (4, a_v), (6, b_exp, 0), (4, a_sums), (4, a_rot),
            (3, a_rt), (2, pre_y), (3, a_hT), (13, parity(c_zT, 0)), (6, b_exp, 1), (1, pre_mm), (0, pre_norm), (0, load_x),
            (14, load_x1), (1, load_tab), (1, load_y)]
        loads(0)
        for t in range(U + 16):
            if t + 1 < U:
                loads(t + 1)
            for d, stage, *rest in ORDER:
                if 0 <= t - d < U:
                    stage(t - d, *rest)
            for d, fn in RELOAD.items():
                if t - d == NG - 1:
                    fn(t - d)
        op("sp", None, [M["sto", U - 1], M["sto", U - 2], M["stx", NG - 1], M["stx", NG - 2]])

        block = ctx.enter_context(nc.Block())

        @block.sync
        def _(e):
            Q.run("sp", e)

        @block.tensor
        def _(e):
            Q.run("pe", e)

        @block.scalar
        def _(e):
            Q.run("act", e)

        @block.vector
        def _(e):
            Q.run("dve", e)

        @block.gpsimd
        def _(e):
            Q.run("pool", e)


def constants():
    f = np.float32
    half = np.arange(0, 64, 2, dtype=f)
    inv = (f(1.0) / np.power(f(10000.0), half / f(64))).astype(f)
    t = np.arange(T, dtype=f)
    fr = t[:, None] * inv[None, :]
    fr = np.concatenate([fr, fr], -1).astype(np.float64)
    base = ((half + f(0.4 * 64)) / f(1.4 * 64)).astype(f)
    power = ((t - f(T // 2)) / f(64.0)).astype(f)
    scale = base.astype(np.float64)[None, :] ** power.astype(np.float64)[:, None]
    scale = np.concatenate([scale, scale], -1)
    sgn = np.concatenate([-np.ones(32), np.ones(32)])[None, :]
    cos, sin = np.cos(fr), np.sin(fr) * sgn
    tab = np.concatenate([cos * scale, sin * scale, cos / scale, sin / scale], -1).astype(f)
    ident = np.eye(128, dtype=f)
    grp = np.kron(np.eye(8), np.full((16, 16), 1.0 / 16)).astype(f)
    i, j = np.arange(128)[:, None], np.arange(128)[None, :]
    cur = np.where(i >= j, 0.0, MASKED)
    prv = np.where(i <= j, 0.0, MASKED)
    mask = np.zeros((128, 2, 256), f)
    mask[:, 0, 0:128], mask[:, 0, 128:256] = cur, prv
    mask[:, 1, 128:256], mask[:, 1, 0:128] = cur, prv
    return tab, ident, grp, mask


def kernel(**inputs):
    import numpy as _np
    import concourse.bacc as _bacc
    from concourse import mybir as _mybir
    from concourse.bass_utils import run_bass_kernel_spmd as _run

    a = {k: _np.asarray(v) for k, v in inputs.items()}

    def per_partition(v):
        return v.reshape(-1, 128).T

    vec = _np.zeros((128, NVEC), _np.float32)
    for name, key in (("mix_r", "L0_attn_time_mix_r"), ("mix_k", "L0_attn_time_mix_k"),
                      ("mix_v", "L0_attn_time_mix_v"), ("decay", "L0_attn_time_decay"),
                      ("first", "L0_attn_time_first"), ("gamma", "L0_attn_ln_gamma"), ("beta", "L0_attn_ln_beta")):
        vec[:, VEC[name]:VEC[name] + 2] = per_partition(a[key].reshape(-1))
    vec[:, VEC["lg"]:VEC["lg"] + 4] = per_partition(a["L0_ffn_ln_g"].reshape(-1))
    vec[:, VEC["lb"]:VEC["lb"] + 4] = per_partition(a["L0_ffn_ln_b"].reshape(-1))
    for l in range(2):
        b1 = a["L0_ffn_b1"][l]
        for name, o, row in (("b1a", 0, 0), ("b1g", HID, 64)):
            c = VEC[name] + 6 * l
            vec[:, c:c + 5] = per_partition(b1[o:o + 640])
            vec[row:row + TAIL, c + 5] = b1[o + 640:o + HID]
    qs, ks = a["L0_ffn_q_scale"], a["L0_ffn_k_scale"]
    row = _np.concatenate([qs, _np.roll(qs, 32, 1), ks, _np.roll(ks, 32, 1)], 1)
    qsk = _np.ascontiguousarray(_np.broadcast_to(row[None], (128, 2, 256)))
    wrkvo = _np.stack([a["L0_attn_W_" + n].T for n in "rkvo"])
    tab, ident, grp, mask = constants()
    arrays = {"x": a["L0_attn_x"], "wrkvo": wrkvo, "wqkv": a["L0_ffn_wqkv"], "wo": a["L0_ffn_wo"],
              "w1": a["L0_ffn_w1"], "w2": a["L0_ffn_w2"], "b2": a["L0_ffn_b2"], "vec": vec, "qsk": qsk, "tab": tab,
              "ident_d": ident, "grp_d": grp, "mask_d": mask}
    arrays = {k: _np.ascontiguousarray(v) for k, v in arrays.items()}
    nc = _bacc.Bacc("TRN2", target_bir_lowering=False, num_devices=1)
    args = {k: nc.dram_tensor(k, v.shape, _mybir.dt.from_np(v.dtype), kind="ExternalInput").ap()
            for k, v in arrays.items()}
    o = nc.dram_tensor("out_dram", (NB, T, C), _mybir.dt.float32, kind="ExternalOutput").ap()
    build(nc, out=o, **args)
    r = _run(nc, [arrays], core_ids=[0])
    return r.results[0]["out_dram"]
```

```python
from contextlib import ExitStack

import numpy as np
import concourse.bass as bass
from concourse import mybir

F32 = mybir.dt.float32
F32R = mybir.dt.float32r
ALU = mybir.AluOpType
ACT = mybir.ActivationFunctionType
AX_X = mybir.AxisListType.X

NB = 2
T = 4096
NWIN = T // 128
NG = NB * NWIN
C = 256
CH = 256
NCH = T // CH
HID = 682
TAIL = HID - 5 * 128
STK = 64 + TAIL + 1
LOW = -1.0e38
MASKED = -1.0e30
EPS_W = 1e-8
EPS_LN = 1e-5

VEC = {"mix_r": 0, "mix_k": 2, "mix_v": 4, "decay": 6, "first": 8, "gamma": 10, "beta": 12,
       "lg": 14, "lb": 18, "b1a": 22, "b1g": 34}
NVEC = 46


class Queues:

    def __init__(self, nc, ctx):
        self.nc, self.ctx = nc, ctx
        self.sems, self.count = {}, {}
        self.q = {"pe": [], "act": [], "dve": [], "pool": [], "sp": []}

    def op(self, eng, fn, waits=(), sig=None, by=1):
        mark = None
        if sig is not None:
            if sig not in self.sems:
                self.sems[sig] = self.ctx.enter_context(self.nc.semaphore(sig))
                self.count[sig] = 0
            self.count[sig] += by
            mark = (sig, self.count[sig])
        self.q[eng].append((fn, [w for w in waits if w is not None], sig, by))
        return mark

    def run(self, eng, e):
        seen = {}
        for fn, waits, sig, by in self.q[eng]:
            for s, v in waits:
                if seen.get(s, 0) < v:
                    e.wait_ge(self.sems[s], v)
                    seen[s] = v
            if fn is None:
                continue
            ins = fn(e)
            if sig is not None:
                ins.then_inc(self.sems[sig], by)


def build(nc, x, wrkvo, wqkv, wo, w1, w2, b2, vec, qsk, tab, ident_d, grp_d, mask_d, out):
    ctx = ExitStack()
    with ctx:
        Q = Queues(nc, ctx)
        op = Q.op
        rwkv_d = nc.dram_tensor("rwkv_scratch", (NB, 2, 128, T), F32, kind="Internal").ap()
        x1_d = nc.dram_tensor("x1_scratch", (NB, T, C), F32, kind="Internal").ap()
        y_d = nc.dram_tensor("y_scratch", (NB, T, C), F32, kind="Internal").ap()

        def sb(name, shape, c=ctx, dt=F32):
            return c.enter_context(nc.sbuf_tensor(name, [128] + shape, dt))

        def pair(name, shape):
            return [sb(name + p, shape, dt=F32R) for p in "hl"]

        def weight_scratch(name, shape):
            return [nc.dram_tensor(name + p, tuple([128] + shape), F32, kind="Internal").ap() for p in "hl"]

        wq_d = weight_scratch("wq_scratch", [2, 1536])
        wo_d = weight_scratch("wo_scratch", [4, 256])
        w1_d = weight_scratch("w1_scratch", [2, 1386])
        w2_d = weight_scratch("w2_scratch", [6, 256])

        PS = ctx.enter_context(nc.psum_tensor("ps", [128, 8, 512], F32))

        ident = sb("ident", [128])
        vecs = sb("vecs", [NVEC])
        Wp = pair("Wp", [2, 256])
        WQ = pair("WQ", [2, 1536])
        WO = pair("WO", [4, 256])
        W1 = pair("W1", [2, 1386])
        W2 = pair("W2", [6, 256])
        wdec = sb("wdec", [2])
        wu = sb("wu", [2])
        epsw = sb("epsw", [1])
        mhalf = sb("mhalf", [16])
        gsc = sb("gsc", [NB, 2])
        gsh = sb("gsh", [NB, 2])

        def V(name, i):
            return vecs[:, VEC[name] + i:VEC[name] + i + 1]

        def dma(dst, src, waits, sig):
            return op("sp", lambda e: e.dma_start(dst, src), waits, sig, 16)

        dma(ident[:, :], ident_d, [], "ld0")
        LD0 = dma(vecs[:, :], vec, [], "ld0")

        MH = op("pool", lambda e: e.memset(mhalf[:, :], -0.5), [], "mh")

        def inv_sqrt(ap, src, sig):
            w = ap.shape[-1]
            return op("pool", lambda e: e.tensor_tensor(ap, ap, mhalf[:, 0:w], ALU.pow), [src, MH], sig)

        EPSM = op("dve", lambda e: e.memset(epsw[:, :], EPS_W), [], "cst")
        m = op("act", lambda e: e.activation(wdec[:, :], vecs[:, VEC["decay"]:VEC["decay"] + 2], ACT.Exp),
               [LD0], "wdec_e")
        m = op("dve", lambda e: e.tensor_scalar(wdec[:, :], wdec[:, :], -1.0, None, ALU.mult), [m, LD0], "wdec")
        WU = op("dve", lambda e: e.tensor_tensor(wu[:, :], wdec[:, :], vecs[:, VEC["first"]:VEC["first"] + 2],
                                                 ALU.add), [m], "wdec")

        held = [[] for _ in range(8)]
        turn = [0]

        def bank():
            b = turn[0] % 8
            turn[0] += 1
            free, held[b] = held[b], None
            return b, list(free)

        def before(name, n, *rest):
            return M[(name, n, *rest)] if n >= 0 else None

        with ExitStack() as c1:
            xc = sb("xc", [4, 2, 256], c1)
            mvs = sb("mvs", [2, 2, 6], c1)
            mva = sb("mva", [2, 2, 2], c1)
            rsd = sb("rsd", [2, 2], c1)
            xT = sb("xT", [2, 2, CH + 1], c1)
            kS = sb("kS", [5, 2, CH], c1)
            vS = sb("vS", [6, 2, CH], c1)
            sg = sb("sg", [8, 2, CH], c1)
            mS = sb("mS", [4, 2, CH + 1], c1)
            bS = sb("bS", [3, 2, CH + 1], c1)
            aS = sb("aS", [2, 2, CH + 1], c1)
            Bc = sb("Bc", [NB, 2], c1)
            q1 = sb("q1", [2, 2, CH], c1)
            km = sb("km", [2, 2, CH], c1)
            BS = sb("BS", [2, 2, CH], c1)
            q2 = sb("q2", [2, CH], c1)
            f = sb("f", [2, 4, 2, CH], c1)
            n2 = sb("n2", [2, 2, CH], c1)
            num = sb("num", [2, 2, CH], c1)
            den = sb("den", [2, 2, CH], c1)
            rw = sb("rw", [2, 2, CH], c1)
            gmv = sb("gmv", [NB, 2, 2], c1)
            gtm = sb("gtm", [NB, 2, 4], c1)
            raw = sb("raw", [2, 768], c1)
            Wc = sb("Wc", [3, 2, 256], c1)
            Wp1 = sb("Wp1", [3, 2, 256], c1)
            grp = sb("grp", [128], c1)
            bst = sb("bst", [NB, 2, NCH, 6], c1)
            wpf = sb("wpf", [2, 256], c1)
            dma(grp[:, :], grp_d, [], "ldw")
            dma(wpf[:, :, :], wrkvo[3].rearrange("(k p) n -> p k n", p=128), [], "ldw")
            LDW = dma(Wp1[:, :, :, :].rearrange("p m k n -> p (m k) n"),
                      wrkvo[0:3].rearrange("m (k p) n -> p (m k) n", p=128), [], "ldw")

            for m_, name in enumerate(("mix_r", "mix_k", "mix_v")):
                for c in range(2):
                    w = op("dve", lambda e, m_=m_, c=c, name=name: e.tensor_scalar(
                        Wc[:, m_, c, :], Wp1[:, m_, c, :], V(name, c), None, ALU.mult), [LDW, LD0], "wmix")
                    WMIX = op("dve", lambda e, m_=m_, c=c: e.tensor_tensor(
                        Wp1[:, m_, c, :], Wp1[:, m_, c, :], Wc[:, m_, c, :], ALU.subtract), [w], "wmix")

            op("dve", lambda e: e.memset(xT[:, :, :, 0:1], 0.0), [], "cst")
            op("dve", lambda e: e.memset(mS[:, :, :, 0:1], LOW), [], "cst")
            op("dve", lambda e: e.memset(aS[:, :, :, 0:1], 0.0), [], "cst")
            op("dve", lambda e: e.memset(Bc[:, :, :], 0.0), [], "cst")
            CST = op("dve", lambda e: e.memset(bS[:, :, :, 0:1], LOW), [], "cst")

            w = op("act", lambda e: e.activation(Wp[0][:, :, :], wpf[:, :, :], ACT.Copy), [LDW], "wps")
            WPS = op("pool", lambda e: e.tensor_tensor(Wp[1][:, :, :], wpf[:, :, :], Wp[0][:, :, :].bitcast(F32),
                                                       ALU.subtract), [w, LDW], "wps2")
            W2Z = op("pool", lambda e: e.memset(W2[0][:, 5, :].bitcast(F32), 0.0), [], "w2z")

            M = {}
            chunks = [(b, j) for j in range(NCH) for b in range(NB)]
            N = len(chunks)

            def load_chunk(n):
                b, j = chunks[n]
                M["ldx", n] = dma(xc[:, n % 4, :, :],
                                  x[b, j * CH:(j + 1) * CH, :].rearrange("(w p) c -> p w c", p=128),
                                  [before("xtr", n - 4)], f"ldx{n % 4}")

            def r_stats(n):
                p = n % 2
                for w in range(2):
                    s = op("dve", lambda e, w=w: e.bn_stats(mvs[:, p, w, :], xc[:, n % 4, w, :]),
                           [M["ldx", n], before("xn", n - 2)], "a_st")
                    g = op("dve", lambda e, w=w: e.bn_aggr(mva[:, p, w, :], mvs[:, p, w, :]), [s], "a_ag")
                r = op("dve", lambda e: e.tensor_scalar(rsd[:, p, :], mva[:, p, :, 1], EPS_LN, None, ALU.add),
                       [g], "a_rs")
                M["rsd", n] = inv_sqrt(rsd[:, p, :], r, "a_rq")

            def r_norm(n):
                p = n % 2
                for w in range(2):
                    M["xn", n] = op("dve", lambda e, w=w: e.tensor_scalar(
                        xc[:, n % 4, w, :], xc[:, n % 4, w, :], mva[:, p, w, 0:1], rsd[:, p, w:w + 1],
                        ALU.subtract, ALU.mult), [M["rsd", n]], "xn")

            def r_turn(n):
                p = n % 2
                k, free = bank()
                for c in range(2):
                    for w in range(2):
                        M["xtr", n] = op("pe", lambda e, c=c, w=w: e.transpose(
                            PS[:, k, c * 256 + w * 128:c * 256 + (w + 1) * 128],
                            xc[:, n % 4, w, c * 128:(c + 1) * 128], ident[:, :]),
                            [M["xn", n], LD0] + free, "xtr" if (c, w) == (1, 1) else None)
                last = None
                used = before("rkv", n - 2, 1)
                if n >= 2:
                    last = op("act", lambda e: e.activation(xT[:, p, :, 0:1], xT[:, p, :, CH:CH + 1], ACT.Copy),
                              [used, M["xT", n - 2]], "xTc")
                M["xT", n] = op("act", lambda e: e.activation(
                    xT[:, p, :, 1:CH + 1], PS[:, k, :].rearrange("p (c t) -> p c t", c=2), ACT.Copy),
                    [M["xtr", n], last, used, CST], "xT")
                held[k] = [M["xT", n]]

            def r_rkv(n):
                p = n % 2
                for i, wsel, dst, fn, R, last in ((2, 0, sg, ACT.Sigmoid, 8, "ns"), (0, 1, kS, ACT.Copy, 5, "q2"),
                                                  (1, 2, vS, ACT.Copy, 6, "n2")):
                    k, free = bank()
                    for g in range(2):
                        for c in range(2):
                            for a, W in enumerate((Wp1, Wc)):
                                M["rkv", n, i] = op("pe", lambda e, g=g, c=c, a=a, W=W, k=k, wsel=wsel: e.matmul(
                                    PS[:, k, g * 256:(g + 1) * 256], W[:, wsel, c, g * 128:(g + 1) * 128],
                                    xT[:, p, c, a:a + CH], start=(c + a == 0), stop=(c + a == 2)),
                                    [M["xT", n], WMIX] + free, "rkv" if (g, c, a) == (1, 1, 1) else None)
                    ws = [M["rkv", n, i], before(last, n - R)] + ([before("evv", n - R)] if i == 1 else [])
                    M["ev", n, i] = op("act", lambda e, k=k, dst=dst, fn=fn, R=R: e.activation(
                        dst[:, n % R, :, :], PS[:, k, :].rearrange("p (g t) -> p g t", g=2), fn), ws, "ev")
                    held[k] = [M["ev", n, i]]

            def r_carry_max(n):
                if n >= 2:
                    M["msc0", n] = op("pool", lambda e: e.tensor_copy(mS[:, n % 4, :, 0:1],
                                                                      mS[:, (n - 2) % 4, :, CH:CH + 1]),
                                      [M["msc", n - 2], before("q1", n - 4)], "msc0")

            def r_carry_acc(n):
                p = n % 2
                if n >= 2:
                    M["asc0", n] = op("pool", lambda e: e.tensor_copy(aS[:, p, :, 0:1], aS[:, p, :, CH:CH + 1]),
                                      [M["asc", n - 2], M["n1", n - 2]], "asc0")

            def r_max(n):
                s, p = n % 4, n % 2
                c = M.get(("msc0", n))
                for g in range(2):
                    M["msc", n] = op("dve", lambda e, g=g: e.tensor_tensor_scan(
                        mS[:, s, g, 1:CH + 1], wdec[:, g:g + 1].broadcast_to([128, CH]), kS[:, n % 5, g, :],
                        mS[:, s, g, 0:1], ALU.add, ALU.max), [M["ev", n, 0], c, WU, CST, before("bS", n - 4)], "msc")
                for g in range(2):
                    M["q1", n] = op("dve", lambda e, g=g: e.scalar_tensor_tensor(
                        out=q1[:, p, g, :], in0=mS[:, s, g, 0:CH], scalar=wdec[:, g:g + 1], in1=mS[:, s, g, 1:CH + 1],
                        op0=ALU.add, op1=ALU.subtract), [M["msc", n], before("bsc", n - 2)], "q1")
                M["km", n] = op("pool", lambda e: e.tensor_tensor(km[:, p, :, :], kS[:, n % 5, :, :],
                                                                  mS[:, s, :, 1:CH + 1], ALU.subtract),
                                [M["msc", n], before("bsc", n - 2)], "km")

            def r_weights(n):
                p = n % 2
                M["ec", n] = op("act", lambda e: e.activation(q1[:, p, :, :], q1[:, p, :, :], ACT.Exp),
                                [M["q1", n]], "ec")
                M["ed", n] = op("act", lambda e: e.activation(km[:, p, :, :], km[:, p, :, :], ACT.Exp),
                                [M["km", n]], "ed")

            def r_sum(n):
                b, p = chunks[n][0], n % 2
                for g in range(2):
                    M["bsc", n] = op("dve", lambda e, g=g: e.tensor_tensor_scan(
                        BS[:, p, g, :], q1[:, p, g, :], km[:, p, g, :], Bc[:, b, g:g + 1], ALU.mult, ALU.add),
                        [M["ec", n], M["ed", n], before("Bc", n - 2), before("bS", n - 2), CST], "bsc")
                M["Bc", n] = op("dve", lambda e: e.tensor_copy(Bc[:, b, :], BS[:, p, :, CH - 1]), [M["bsc", n]], "Bc")

            def r_log(n):
                p, s = n % 2, n % 3
                M["lB", n] = op("act", lambda e: e.activation(BS[:, p, :, :], BS[:, p, :, :], ACT.Ln,
                                                              bias=epsw[:, 0:1]), [M["Bc", n], EPSM], "lB")
                c = None
                if n >= 2:
                    c = op("pool", lambda e: e.tensor_copy(bS[:, s, :, 0:1], bS[:, (n - 2) % 3, :, CH:CH + 1]),
                           [M["bS", n - 2], before("q2", n - 3)], "bSc")
                M["bS", n] = op("pool", lambda e: e.tensor_tensor(bS[:, s, :, 1:CH + 1], mS[:, n % 4, :, 1:CH + 1],
                                                                  BS[:, p, :, :], ALU.add),
                                [M["lB", n], c, before("q2", n - 3), CST], "bS")

            def r_q(n):
                s, p = n % 3, n % 2
                for g in range(2):
                    M["q2", n] = op("dve", lambda e, g=g: e.scalar_tensor_tensor(
                        out=q2[:, g, :], in0=bS[:, s, g, 0:CH], scalar=wdec[:, g:g + 1], in1=kS[:, n % 5, g, :],
                        op0=ALU.add, op1=ALU.subtract), [M["bS", n], before("f", n - 1, 2)], "q2")
                used = [M["q2", n], before("dn", n - 2), before("n1", n - 2), before("n2", n - 2)]
                for i, o in ((1, ALU.max), (0, ALU.min)):
                    M["f", n, i] = op("dve", lambda e, i=i, o=o: e.tensor_scalar(f[:, p, i, :, :], q2[:, :, :], 0.0,
                                                                                 None, o), used, "f")
                for i, o in ((3, ALU.max), (2, ALU.min)):
                    for g in range(2):
                        M["f", n, i] = op("dve", lambda e, i=i, g=g, o=o: e.tensor_scalar(
                            f[:, p, i, g, :], q2[:, g, :], wu[:, g:g + 1], 0.0, ALU.subtract, o), used, "f")

            def r_exps(n):
                p = n % 2
                for i, sc_ in ((1, -1.0), (3, -1.0), (0, 1.0), (2, 1.0)):
                    M["xe", n, i] = op("act", lambda e, i=i, sc_=sc_: e.activation(
                        f[:, p, i, :, :], f[:, p, i, :, :], ACT.Exp, scale=sc_), [M["f", n, i]], "xe")
                M["evv", n] = op("pool", lambda e: e.tensor_tensor(f[:, p, 1, :, :], f[:, p, 1, :, :],
                                                                   vS[:, n % 6, :, :], ALU.mult), [M["xe", n, 1]], "evv")
                M["n2", n] = op("pool", lambda e: e.tensor_tensor(n2[:, p, :, :], f[:, p, 3, :, :], vS[:, n % 6, :, :],
                                                                  ALU.mult), [M["xe", n, 3], before("num", n - 2)], "n2")

            def r_acc(n):
                p = n % 2
                c = M.get(("asc0", n))
                for g in range(2):
                    M["asc", n] = op("dve", lambda e, g=g: e.tensor_tensor_scan(
                        aS[:, p, g, 1:CH + 1], f[:, p, 0, g, :], f[:, p, 1, g, :], aS[:, p, g, 0:1], ALU.mult, ALU.add),
                        [M["xe", n, 0], M["evv", n], c, CST], "asc")
                M["dn", n] = op("dve", lambda e: e.scalar_tensor_tensor(
                    out=den[:, p, :, :], in0=f[:, p, 2, :, :], scalar=epsw[:, 0:1], in1=f[:, p, 3, :, :],
                    op0=ALU.add, op1=ALU.add), [M["xe", n, 2], M["xe", n, 3], EPSM, before("rw", n - 2)], "dn")
                M["n1", n] = op("dve", lambda e: e.tensor_tensor(num[:, p, :, :], f[:, p, 2, :, :], aS[:, p, :, 0:CH],
                                                                 ALU.mult),
                                [M["xe", n, 2], M["asc", n], before("rw", n - 2)], "n1")

            def r_logden(n):
                p = n % 2
                M["ld", n] = op("act", lambda e: e.activation(den[:, p, :, :], den[:, p, :, :], ACT.Ln), [M["dn", n]],
                                "ld")

            def r_recip(n):
                p = n % 2
                M["rd", n] = op("act", lambda e: e.activation(den[:, p, :, :], den[:, p, :, :], ACT.Exp, scale=-1.0),
                                [M["ld", n]], "rd")

            def r_gate(n):
                p = n % 2
                M["num", n] = op("pool", lambda e: e.tensor_tensor(num[:, p, :, :], num[:, p, :, :], n2[:, p, :, :],
                                                                   ALU.add), [M["n1", n], M["n2", n]], "num")
                M["ns", n] = op("pool", lambda e: e.tensor_tensor(num[:, p, :, :], num[:, p, :, :], sg[:, n % 8, :, :],
                                                                  ALU.mult), [M["num", n], M["ev", n, 2]], "ns")

            def r_out(n):
                b, j = chunks[n]
                p = n % 2
                M["rw", n] = op("dve", lambda e: e.tensor_tensor(rw[:, p, :, :], num[:, p, :, :], den[:, p, :, :],
                                                                 ALU.mult),
                                [M["ns", n], M["rd", n], before("str", n - 2), before("bst", n - 2)], "rw")
                for g in range(2):
                    M["bst", n] = op("dve", lambda e, g=g: e.bn_stats(bst[:, b, g, j, :], rw[:, p, g, :]),
                                     [M["rw", n]], "bst")
                M["str", n] = dma(rwkv_d[b, :, :, j * CH:(j + 1) * CH].rearrange("g p t -> p g t"), rw[:, p, :, :],
                                  [M["rw", n]], f"str{p}")

            def weight_pieces(l):
                w = w1[l].rearrange("(k p) n -> p k n", p=128)
                A, tl = slice(0, 128), slice(0, TAIL)
                ps = [(WQ, lambda t, k=k, o=o: t[:, k, o:o + 768], A, 768,
                       [(A, 0, 768, wqkv[l, k * 128:(k + 1) * 128, o:o + 768], 0)])
                      for k in range(2) for o in (0, 768)]
                ps += [(WO, lambda t, k=k: t[:, k:k + 2, :].rearrange("p k n -> p (k n)"), A, 512,
                        [(A, 0, 512, wo[l, k * 128:(k + 2) * 128, :].rearrange("(k p) n -> p k n", p=128), 2)])
                       for k in (0, 2)]
                for k in range(2):
                    ps.append((W1, lambda t, k=k: t[:, k, 0:640], A, 640, [(A, 0, 640, w[:, k, 0:640], 0)]))
                    ps.append((W1, lambda t, k=k: t[:, k, 640:1386], A, 746,
                               [(A, 0, 640, w[:, k, HID:HID + 640], 0), (A, 640, TAIL, w[:, k, 640:HID], 0),
                                (A, 704, TAIL, w[:, k, HID + 640:2 * HID], 0)]))
                ps += [(W2, lambda t, k=k, m=m: t[:, k:k + m, :].rearrange("p k n -> p (k n)"), A, m * 256,
                        [(A, 0, m * 256, w2[l, k * 128:(k + m) * 128, :].rearrange("(k p) n -> p k n", p=128), m)])
                       for k, m in ((0, 3), (3, 2))]
                ps.append((W2, lambda t: t[0:TAIL + 1, 5, :], slice(0, TAIL + 1), 256,
                           [(tl, 0, 256, w2[l, 640:HID, :], 0), (slice(TAIL, TAIL + 1), 0, 256, b2[l:l + 1, :], 0)]))
                return ps

            half = len(weight_pieces(0))
            LW = {}

            def load_piece(i):
                l, (tiles, view, rows, n, parts) = todo[i]
                used = SPLIT[i - 2] if i >= 2 else None
                zero = None
                if n == 746:
                    zero = op("pool", lambda e: e.memset(raw[:, i % 2, 640 + TAIL:704], 0.0), [used], "w_z")
                for r, c, w, src, k in parts:
                    dst = raw[r, i % 2, c:c + w]
                    m = dma(dst.rearrange("p (k n) -> p k n", k=k) if k else dst, src, [used], f"w_ld{i % 2}")
                LW[i] = [m, zero]

            def split_piece(i):
                l, (tiles, view, rows, n, parts) = todo[i]
                src = raw[rows, i % 2, 0:n]
                ws = LW[i] + ([] if l else [WST])
                h = op("act", lambda e: e.activation(view(tiles[0]), src, ACT.Copy), ws + [W2Z], "w_hi")
                if n == 256:
                    h = op("act", lambda e: e.activation(W2[0][64:STK, 5, :], src, ACT.Copy), ws + [W2Z], "w_hi")
                SPLIT.append(op("pool", lambda e: e.tensor_tensor(view(tiles[1]), src, view(tiles[0]).bitcast(F32),
                                                                  ALU.subtract), ws + [h], "w_lo"))

            def store_layer():
                for a in (0, 1):
                    for d, t in ((wq_d, WQ), (wo_d, WO), (w1_d, W1)):
                        dma(d[a], t[a][:, :, :].bitcast(F32), [SPLIT[-1]], "w_st")
                    dma(w2_d[a][:, 0:5, :], W2[a][:, 0:5, :].bitcast(F32), [SPLIT[-1]], "w_st")
                    r = slice(0, TAIL + 1 if a else STK)
                    m = dma(w2_d[a][r, 5, :], W2[a][r, 5, :].bitcast(F32), [SPLIT[-1]], "w_st")
                return m

            ORDER1 = [(11, r_logden), (7, r_log), (11, r_gate), (12, r_out),
                      (9, r_exps), (5, r_weights), (11, r_recip), (10, r_acc), (8, r_q), (6, r_sum), (4, r_max),
                      (2, r_turn), (3, r_rkv), (1, r_norm), (3, r_carry_max), (9, r_carry_acc),
                      (0, r_stats)]
            todo = [(l, p) for l in (1, 0) for p in weight_pieces(l)]
            split_load = {(1 if i < half else 5) + i: i for i in range(2 * half)}
            SPLIT = []
            WST = None
            load_chunk(0)
            load_chunk(1)
            for t in range(N + 13):
                for d, stage in ORDER1:
                    if 0 <= t - d < N:
                        stage(t - d)
                if t + 2 < N:
                    load_chunk(t + 2)
                if t - 1 in split_load:
                    split_piece(split_load[t - 1])
                    if len(SPLIT) == half:
                        WST = store_layer()
                if t in split_load:
                    load_piece(split_load[t])
            SPLIT_DONE = [SPLIT[-1], WST]

            for b in range(NB):
                for g in range(2):
                    m = op("dve", lambda e, b=b, g=g: e.bn_aggr(
                        gmv[:, b, g, :], bst[:, b, g, :, :].rearrange("p j s -> p (j s)")), [M["bst", N - 1]], "gag")
            G1 = op("pe", lambda e: e.matmul(PS[:, 0, 0:4], grp[:, :], gmv[:, :, :, 0].rearrange("p b g -> p (b g)"),
                                             start=True, stop=True), [m, M["xT", N - 1], M["ev", N - 1, 1], LDW], "g1")
            m = op("dve", lambda e: e.tensor_copy(gtm[:, :, :, 0], PS[:, 0, 0:4].rearrange("p (b g) -> p b g", b=2)),
                   [G1], "g2")
            m = op("dve", lambda e: e.tensor_tensor(gtm[:, :, :, 1], gmv[:, :, :, 0], gtm[:, :, :, 0], ALU.subtract),
                   [m], "g2")
            m = op("dve", lambda e: e.tensor_tensor(gtm[:, :, :, 2], gtm[:, :, :, 1], gtm[:, :, :, 1], ALU.mult),
                   [m], "g2")
            m = op("dve", lambda e: e.tensor_tensor(gtm[:, :, :, 3], gtm[:, :, :, 2], gmv[:, :, :, 1], ALU.add),
                   [m], "g2")
            G3 = op("pe", lambda e: e.matmul(PS[:, 1, 0:4], grp[:, :], gtm[:, :, :, 3].rearrange("p b g -> p (b g)"),
                                             start=True, stop=True), [m], "g1")
            m = op("dve", lambda e: e.tensor_scalar(gsc[:, :, :], PS[:, 1, 0:4].rearrange("p (b g) -> p b g", b=2),
                                                    EPS_LN, None, ALU.add), [G3], "g2")
            m = inv_sqrt(gsc[:, :, :].rearrange("p b g -> p (b g)"), m, "g4")
            for b in range(NB):
                m2 = op("dve", lambda e, b=b: e.tensor_tensor(gsc[:, b, :], gsc[:, b, :],
                                                              vecs[:, VEC["gamma"]:VEC["gamma"] + 2], ALU.mult),
                        [m], "g2")
            m = op("dve", lambda e: e.tensor_tensor(gtm[:, :, :, 1], gtm[:, :, :, 0], gsc[:, :, :], ALU.mult),
                   [m2], "g2")
            for b in range(NB):
                GN = op("dve", lambda e, b=b: e.tensor_tensor(gsh[:, b, :], vecs[:, VEC["beta"]:VEC["beta"] + 2],
                                                              gtm[:, b, :, 1], ALU.subtract), [m], "g2")
            STORED = [M["str", N - 1], M["str", N - 2]]

        U = 2 * NG
        NY, NV, NX = 8, 5, 7
        mask = sb("mask", [2, 256])
        qsks = sb("qsks", [2, 256])
        xin = sb("xin", [2, 256])
        rk = sb("rk", [2, 2, 128])
        nF = sb("nF", [2, 128])
        nT = pair("nT", [2, 128])
        x1 = sb("x1", [2, 256])
        x1i = sb("x1i", [2, 256])
        st0 = sb("st0", [6])
        mv0 = sb("mv0", [2])
        r0 = sb("r0", [1])
        y = sb("y", [NY, 256])
        tb = sb("tb", [2, 256])
        rt = sb("rt", [2, 256])
        hT = pair("hT", [2, 129])
        sq = sb("sq", [1024])
        ss = sb("ss", [16])
        rs = sb("rs", [2, 16])
        sc = sb("sc", [4, 8])
        Ar = sb("Ar", [1024])
        Br = sb("Br", [1024])
        qT = pair("qT", [4, 128])
        kh = sb("kh", [4, 128], dt=F32R)
        kl = sb("kl", [2, 4, 128], dt=F32R)
        qq = sb("qq", [2, 4, 128], dt=F32R)
        kk = sb("kk", [2, 2, 4, 128], dt=F32R)
        vv = sb("vv", [NV, 8, 64])
        Sm = sb("Sm", [8, 256])
        mx = sb("mx", [8])
        sm = sb("sm", [2, 8])
        nb = sb("nb", [8])
        PT = sb("PT", [8, 256])
        ro = sb("ro", [8])
        oS = sb("oS", [8, 64])
        oT = pair("oT", [4, 128])
        x2 = sb("x2", [NX, 256])
        h2 = sb("h2", [3, 128])
        st1 = sb("st1", [12])
        mv1 = sb("mv1", [2, 2])
        r1 = sb("r1", [2, 1])
        z = sb("z", [2, 256])
        zf = sb("zf", [2, 2, 128])
        zT = pair("zT", [2, 256])
        Gl = sb("Gl", [4, 256])
        uT = pair("uT", [6, 256])
        os_ = sb("os", [2, 256])

        first = [GN] + STORED + SPLIT_DONE
        op("dve", lambda e: e.memset(uT[0][0:64, 5, :].bitcast(F32), 1.0), first, "end")
        op("dve", lambda e: e.memset(h2[0:1, :, :], 0.0), [], "end")
        END = op("dve", lambda e: e.memset(uT[0][64:128, 5, :].bitcast(F32), 0.0), [], "end")
        for eng in ("pe", "act", "pool", "sp"):
            op(eng, None, [END])
        dma(mask[:, :, :], mask_d, [END], "ld2")
        LD2 = dma(qsks[:, :, :], qsk, [END], "ld2")

        M = {}

        def first_win(n):
            return n % NWIN == 0

        def place(n):
            l, g = divmod(n, NG)
            return l, g, g // NWIN, g % NWIN

        def mm3(dst, L, R, start, stop, waits, sig):
            prods = ((0, 0), (1, 0), (0, 1))
            for i, (a, b) in enumerate(prods):
                last = op("pe", lambda e, a=a, b=b, i=i: e.matmul(dst, L(a), R(b), start=start and i == 0,
                                                                  stop=stop and i == 2),
                          waits, sig if i == 2 else None)
            return last

        def high(dst, src, waits, sig):
            return op("act", lambda e: e.activation(dst, src, ACT.Copy), waits, sig)

        def low(dst, src, hi, waits, sig, eng="dve"):
            return op(eng, lambda e: e.tensor_tensor(dst, src, hi.bitcast(F32), ALU.subtract), waits, sig)

        WREADY = {}

        def loads(n):
            l, g, b, w = place(n)
            rows = slice(w * 128, (w + 1) * 128)
            if l == 0:
                M["lrk", n] = dma(rk[:, n % 2, :, :], rwkv_d[b, :, :, rows].rearrange("g p t -> p g t"),
                                  [before("nF", n - 2)] + STORED, f"lrk{n % 2}")

        def load_x(n):
            l, g, b, w = place(n)
            if l == 0:
                M["lxi", n] = dma(xin[:, n % 2, :], x[b, w * 128:(w + 1) * 128, :], [before("x1", n - 2)],
                                  f"lxi{n % 2}")

        def load_y(n):
            l, g, b, w = place(n)
            rows = slice(w * 128, (w + 1) * 128)
            if l:
                M["y", n] = dma(y[:, n % NY, :], y_d[b, rows, :], [M["x2", n - NY], M["sty", g]], f"ly{n % 4}")

        def load_tab(n):
            l, g, b, w = place(n)
            rows = slice(w * 128, (w + 1) * 128)
            M["ltb", n] = dma(tb[:, n % 2, :], tab[rows, :], [before("rt", n - 2)], f"ltb{n % 2}")

        def load_x1(n):
            l, g, b, w = place(n)
            if l:
                M["lx1", n] = dma(x1i[:, n % 2, :], x1_d[b, w * 128:(w + 1) * 128, :],
                                  [M["stx", g], M["os", n - 2] if g >= 2 else None], f"lx1{n % 2}")

        def pre_norm(n):
            l, g, b, w = place(n)
            if l:
                return
            for c in range(2):
                M["nF", n] = op("act", lambda e, c=c: e.activation(
                    nF[:, c, :], rk[:, n % 2, c, :], ACT.Identity, bias=gsh[:, b, c:c + 1], scale=gsc[:, b, c:c + 1]),
                    [M["lrk", n], before("nT", n - 1), GN], "nF")
            h = high(nT[0][:, :, :], nF[:, :, :], [M["nF", n], before("p0", n - 1)], "nTh")
            M["nT", n] = low(nT[1][:, :, :], nF[:, :, :], nT[0][:, :, :], [h, before("p0", n - 1)], "nTl", "pool")

        def pre_mm(n):
            l, g, b, w = place(n)
            if l:
                return
            k, free = bank()
            for c in range(2):
                M["p0", n] = mm3(PS[:, k, 0:256], lambda a, c=c: nT[a][:, c, :], lambda a, c=c: Wp[a][:, c, :],
                                 c == 0, c == 1, [M["nT", n], WPS] + free, "p0" if c else None)
            a = M["x1", n] = op("dve", lambda e: e.tensor_tensor(x1[:, n % 2, :], PS[:, k, 0:256], xin[:, n % 2, :],
                                                                 ALU.add),
                                [M["p0", n], M["lxi", n], before("y0", n - 2), before("stx", n - 2)], "x1")
            held[k] = [a]
            M["stx", n] = dma(x1_d[b, w * 128:(w + 1) * 128, :], x1[:, n % 2, :], [a], f"stx{n % 2}")
            a = op("dve", lambda e: e.bn_stats(st0[:, 0:6], x1[:, n % 2, :]), [a], "ps")
            a = op("dve", lambda e: e.bn_aggr(mv0[:, :], st0[:, 0:6]), [a, before("y0", n - 1)], "ps")
            a = op("dve", lambda e: e.tensor_scalar(r0[:, :], mv0[:, 1:2], EPS_LN, None, ALU.add), [a], "ps")
            M["r0", n] = inv_sqrt(r0[:, :], a, "r0")

        def pre_y(n):
            if n < NG:
                M["y", n] = M["y0", n] = op("dve", lambda e: e.tensor_scalar(
                    y[:, n % NY, :], x1[:, n % 2, :], mv0[:, 0:1], r0[:, 0:1], ALU.subtract, ALU.mult),
                    [M["r0", n], before("x2", n - NY)], "y0")

        def a_rt(n):
            l = n // NG
            M["rt", n] = op("pool", lambda e: e.tensor_tensor(rt[:, n % 2, :], tb[:, n % 2, :], qsks[:, l, :],
                                                              ALU.mult),
                            [M["ltb", n], LD2, before("rope", n - 2, 0)], "rt")

        def a_hT(n):
            k, free = bank()
            for c in range(2):
                t = op("pe", lambda e, c=c: e.transpose(PS[:, k, c * 128:(c + 1) * 128],
                                                        y[:, n % NY, c * 128:(c + 1) * 128], ident[:, :]),
                       [M["y", n]] + free, "p1" if c else None)
            used = before("p2", n - 1, 2)
            if first_win(n):
                c0 = [op("dve", lambda e, a=a: e.memset(hT[a][:, 1, 0:1].bitcast(F32), 0.0), [used], "hTc") for a in (0, 1)]
            else:
                c0 = [op("act", lambda e: e.activation(hT[0][:, 1, 0:1], hT[0][:, 1, 128:129].bitcast(F32), ACT.Copy),
                         [used, M["hTh", n - 1]], "hTa"),
                      op("dve", lambda e: e.tensor_copy(hT[1][:, 1, 0:1], hT[1][:, 1, 128:129].bitcast(F32)),
                         [used, M["hT", n - 1][-1]], "hTc")]
            src = PS[:, k, 0:256].rearrange("p (c t) -> p c t", c=2)
            h = M["hTh", n] = high(hT[0][:, :, 1:129], src, [t, used] + c0, "hTh")
            lo = low(hT[1][:, :, 1:129], src, hT[0][:, :, 1:129], [h] + c0, "hTl")
            held[k] = [lo]
            M["hT", n] = c0 + [h, lo]

        def a_qkv(n, i):
            l = n // NG
            k, free = bank()
            M["qb", n, i] = k
            for c in range(2):
                M["p2", n, i] = mm3(PS[:, k, :], lambda a, c=c: hT[a][:, c, 1 - c:129 - c],
                                    lambda a, c=c: WQ[a][:, c, i * 512:(i + 1) * 512], c == 0, c == 1,
                                    M["hT", n] + free + [WREADY.get(("q", l))], "p2" if c else None)

        def a_square(n, i):
            k = M["qb", n, i]
            M["sq", n, i] = op("act", lambda e: e.activation(sq[:, i * 512:(i + 1) * 512], PS[:, k, :], ACT.Square),
                               [M["p2", n, i], before("ss", n - 1)], "sq")

        def a_rope(n, i):
            k = M["qb", n, i]
            X = PS[:, k, :].rearrange("p (h d) -> p h d", h=8)
            A = Ar[:, i * 512:(i + 1) * 512].rearrange("p (h d) -> p h d", h=8)
            B = Br[:, i * 512:(i + 1) * 512].rearrange("p (h d) -> p h d", h=8)
            t0 = rt[:, n % 2, i * 128:i * 128 + 64].unsqueeze(1)
            t1 = rt[:, n % 2, i * 128 + 64:i * 128 + 128].unsqueeze(1)
            ws = [M["sq", n, i], M["rt", n], before("p3", n - 1, i), before("kr" if i else "qr", n - 1)]
            op("dve", lambda e: e.tensor_tensor(A, X, t0.broadcast_to([128, 8, 64]), ALU.mult), ws)
            op("dve", lambda e: e.tensor_tensor(B[:, :, 0:32], X[:, :, 32:64],
                                                t1[:, :, 0:32].broadcast_to([128, 8, 32]), ALU.mult), ws)
            M["rope", n, i] = op("dve", lambda e: e.tensor_tensor(
                B[:, :, 32:64], X[:, :, 0:32], t1[:, :, 32:64].broadcast_to([128, 8, 32]), ALU.mult), ws, "rope")
            held[k] = [M["rope", n, i]]

        def a_v(n):
            k = M["qb", n, 2]
            src = PS[:, k, :].rearrange("p (h d) -> p h d", h=8)
            s = n % NV
            used = before("p6", n - NV + 1, 1)
            M["v", n] = high(vv[:, s, :, :], src, [M["p2", n, 2], used], "v")
            held[k] = [M["v", n]]

        def a_sums(n):
            M["ss", n] = op("dve", lambda e: e.tensor_reduce(
                ss[:, :], sq[:, :].rearrange("p (h d) -> p h d", h=16), AX_X, ALU.add),
                [M["sq", n, 0], M["sq", n, 1]], "ss")
            M["rsm", n] = op("dve", lambda e: e.tensor_scalar(rs[:, n % 2, :], ss[:, :], 1e-24, None, ALU.max),
                             [M["ss", n], before("kn", n - 2), before("sc", n - 2)], "rsm")

        def a_rot(n):
            for i, name in ((1, "kr"), (0, "qr")):
                r = slice(i * 512, (i + 1) * 512)
                M[name, n] = op("pool", lambda e, r=r: e.tensor_tensor(Ar[:, r], Ar[:, r], Br[:, r], ALU.add),
                                [M["rope", n, i]], name)

        def a_scale(n):
            M["rs", n] = inv_sqrt(rs[:, n % 2, :], M["rsm", n], "rs")
            A = Ar[:, 512:1024].rearrange("p (h d) -> p h d", h=8)
            M["kn", n] = op("pool", lambda e: e.tensor_tensor(
                A, A, rs[:, n % 2, 8:16].unsqueeze(2).broadcast_to([128, 8, 64]), ALU.mult),
                [M["kr", n], M["rs", n]], "kn")
            M["sc", n] = op("pool", lambda e: e.tensor_scalar(sc[:, n % 4, :], rs[:, n % 2, 0:8], 8.0, None, ALU.mult),
                            [M["rs", n], before("ex", n - 4, 1)], "sc")

        def a_qkT(n, i):
            k, free = bank()
            for c in range(4):
                M["p3", n, i] = op("pe", lambda e, c=c: e.transpose(
                    PS[:, k, c * 128:(c + 1) * 128], Ar[:, i * 512 + c * 128:i * 512 + (c + 1) * 128], ident[:, :]),
                    [M["kn" if i else "qr", n]] + free, "p3" if c == 3 else None)
            M["qkb", n, i] = k

        def a_qkT_parts(n, i):
            k = M["qkb", n, i]
            used = [before("p4", n - 1, 1)] + (before("kqd" if i else "qqd", n - 1) or [])
            d = (kh[:, :, :], kl[:, n % 2, :, :]) if i else (qT[0][:, :, :], qT[1][:, :, :])
            d = [t.rearrange("p c t -> p (c t)") for t in d]
            h = high(d[0], PS[:, k, :], [M["p3", n, i]] + used, "qkh")
            lo = low(d[1], PS[:, k, :], d[0], [h] + used, "qkl")
            held[k] = [lo]
            M["qkT", n, i] = lo

        def a_stack(n, i):
            lo_, hi_ = slice(0, 64), slice(64, 128)
            done = []
            for par, own, other in ((0, lo_, hi_), (1, hi_, lo_)):
                for a, rows in enumerate((own, other)):
                    src = kh if i else qT[a]
                    dst = kk[rows, n % 2, par, :, :] if i else qq[rows, par, :, :]
                    m = dma(dst.bitcast(F32), src[own, :, :].bitcast(F32), [M["qkT", n, i], before("p4", n - 1, 1)],
                            f"stk{i}{n % 2}")
                    done.append(m)
            M["kqd" if i else "qqd", n] = done[-1:]

        def cols(n):
            return (n % 2 * 128, n % 2 * 128 + 128) if first_win(n) else (0, 256)

        def b_scores(n, q):
            c0, c1 = cols(n)
            ks = [bank(), bank()]
            for h in range(4 * q, 4 * q + 4):
                p0 = 64 * (h % 2)
                k, free = ks[h % 2]
                dst = PS[:, k, (h // 2 % 2) * 256 + c0:(h // 2 % 2) * 256 + c1]

                c = h // 2
                side = n % 2 if first_win(n) else slice(0, 2)
                ws = M["kqd", n] + M["qqd", n] + free
                op("pe", lambda e, dst=dst, h=h, c=c, side=side: e.matmul(
                    dst, qq[:, h % 2, c, :], kk[:, side, h % 2, c, :], start=True, stop=False), ws)
                M["p4", n, q] = M["p4", n, q, h % 2] = op("pe", lambda e, dst=dst, p0=p0, c=c, side=side: e.matmul(
                    dst, qT[0][p0:p0 + 64, c, :], kl[p0:p0 + 64, side, c, :], start=False, stop=True),
                    ws, "p4" if h % 4 >= 2 else None)
            for h in (4 * q, 4 * q + 2, 4 * q + 1, 4 * q + 3):
                k = ks[h % 2][0]
                m = op("dve", lambda e, h=h, k=k: e.tensor_tensor_reduce(
                    Sm[:, h, c0:c1], PS[:, k, (h // 2 % 2) * 256 + c0:(h // 2 % 2) * 256 + c1],
                    mask[:, n % 2, c0:c1], 1.0, -3.0e38, ALU.add, ALU.max, mx[:, h:h + 1]),
                    [M["p4", n, q, h % 2], before("p5", n - 1, h // 2), LD2], "mx")
                held[k] = [m]
            M["mx", n, q] = m
            r = slice(4 * q, 4 * q + 4)
            M["nb", n, q] = op("dve", lambda e: e.scalar_tensor_tensor(
                out=nb[:, r], in0=mx[:, r], scalar=-1.0, in1=sc[:, n % 4, r], op0=ALU.mult, op1=ALU.mult),
                [m, M["sc", n], before("ex", n - 1, q)], "nb")

        def b_exp(n, q):
            c0, c1 = cols(n)
            for h in range(4 * q, 4 * q + 4):
                M["ex", n, q] = M["exh", n, h] = op("act", lambda e, h=h: e.activation(
                    Sm[:, h, c0:c1], Sm[:, h, c0:c1], ACT.Exp, bias=nb[:, h:h + 1], scale=sc[:, n % 4, h:h + 1],
                    accum_out=sm[:, n % 2, h:h + 1]), [M["nb", n, q], before("ro", n - 2, q)], "ex")

        def b_turn(n, j):
            c0, c1 = cols(n)
            k, free = bank()
            for i in range(2):
                for c in range(c0, c1, 128):
                    M["p5", n, j] = op("pe", lambda e, i=i, c=c: e.transpose(
                        PS[:, k, i * 256 + c:i * 256 + c + 128], Sm[:, 2 * j + i, c:c + 128], ident[:, :]),
                        [M["exh", n, 2 * j + 1]] + free, "p5" if i and c + 128 == c1 else None)
            used = before("p6", n - 1, j // 2)
            src = PS[:, k, :].rearrange("p (h j) -> p h j", h=2)[:, :, c0:c1]
            M["PT", n, j] = high(PT[:, 2 * j:2 * j + 2, c0:c1], src, [M["p5", n, j], used], "pt")
            held[k] = [M["PT", n, j]]

        def b_pv(n, q):
            sides = [n % 2] if first_win(n) else [1 - n % 2, n % 2]
            k, free = bank()
            ws = [M["PT", n, 2 * q], M["PT", n, 2 * q + 1], M["v", n]] + free
            for i in range(4):
                h = 4 * q + i
                for s in sides:
                    v = n % NV if s == n % 2 else (n - 1) % NV
                    M["p6", n, q] = op("pe", lambda e, i=i, h=h, s=s, v=v: e.matmul(
                        PS[:, k, 64 * i:64 * i + 64], PT[:, h, s * 128:(s + 1) * 128], vv[:, v, h, :],
                        start=s == sides[0], stop=s == sides[-1]), ws, "p6" if i == 3 and s == sides[-1] else None)
            O = PS[:, k, 0:256].rearrange("p (h d) -> p h d", h=4)
            r = slice(4 * q, 4 * q + 4)
            M["ro", n, q] = op("dve", lambda e: e.reciprocal(ro[:, r], sm[:, n % 2, r]),
                               [M["ex", n, q], before("on", n - 1, q)], "ro")
            M["on", n, q] = op("dve", lambda e: e.tensor_tensor(
                oS[:, r, :], O, ro[:, r].unsqueeze(2).broadcast_to([128, 4, 64]), ALU.mult),
                [M["p6", n, q], M["ro", n, q], before("p7", n - 1)], "on")
            held[k] = [M["on", n, q]]

        def c_oT(n):
            k, free = bank()
            for c in range(4):
                M["p7", n] = op("pe", lambda e, c=c: e.transpose(
                    PS[:, k, c * 128:(c + 1) * 128], oS[:, 2 * c:2 * c + 2, :].rearrange("p h d -> p (h d)"),
                    ident[:, :]), [M["on", n, 0], M["on", n, 1]] + free, "p7" if c == 3 else None)
            d = [oT[a][:, :, :].rearrange("p c t -> p (c t)") for a in (0, 1)]
            h = high(d[0], PS[:, k, :], [M["p7", n], before("p8", n - 1)], "oTh")
            M["oT", n] = low(d[1], PS[:, k, :], d[0], [h, before("p8", n - 1)], "oTl")
            held[k] = [M["oT", n]]

        def c_wo(n):
            l = n // NG
            k, free = bank()
            for c in range(4):
                M["p8", n] = mm3(PS[:, k, 0:256], lambda a, c=c: oT[a][:, c, :], lambda a, c=c: WO[a][:, c, :],
                                 c == 0, c == 3, [M["oT", n], WREADY.get(("o", l))] + free, "p8" if c == 3 else None)
            M["x2", n] = op("dve", lambda e: e.tensor_tensor(x2[:, n % NX, :], PS[:, k, 0:256], y[:, n % NY, :],
                                                             ALU.add),
                            [M["p8", n], M["y", n], before("x3", n - NX), before("h2", n - NX + 1)], "x2")
            held[k] = [M["x2", n]]

        def c_shift(n):
            s = n % 3
            ws = [M["x2", n], before("z", n - 3)]
            if first_win(n):
                if n:
                    ws.append(op("dve", lambda e: e.memset(h2[0:1, s, :], 0.0), [before("z", n - 3)], "h2z"))
            else:
                dma(h2[0:1, s, :], x2[127:128, (n - 1) % NX, 128:256], ws, f"h2{s}")
            M["h2", n] = dma(h2[1:128, s, :], x2[0:127, n % NX, 128:256], ws, f"h2{s}")

        def c_stats(n):
            a0 = op("dve", lambda e: e.bn_stats(st1[:, 0:6], x2[:, n % NX, 0:128]), [M["x2", n]], "ls")
            a = op("dve", lambda e: e.bn_stats(st1[:, 6:12], h2[:, n % 3, :]), [M["h2", n]], "ls")
            a = op("dve", lambda e: e.bn_aggr(mv1[:, n % 2, :], st1[:, :]), [a0, a, before("z", n - 2)], "ls")
            a = op("dve", lambda e: e.tensor_scalar(r1[:, n % 2, :], mv1[:, n % 2, 1:2], EPS_LN, None, ALU.add), [a], "ls")
            M["r1", n] = inv_sqrt(r1[:, n % 2, :], a, "r1")

        def c_z(n):
            used = before("p10", n - 2)
            op("dve", lambda e: e.tensor_scalar(z[:, n % 2, 0:128], x2[:, n % NX, 0:128], mv1[:, n % 2, 0:1], r1[:, n % 2, 0:1],
                                                ALU.subtract, ALU.mult), [M["r1", n], M["h2", n], used])
            M["z", n] = op("dve", lambda e: e.tensor_scalar(z[:, n % 2, 128:256], h2[:, n % 3, :], mv1[:, n % 2, 0:1], r1[:, n % 2, 0:1],
                                                            ALU.subtract, ALU.mult), [M["r1", n], used], "z")

        def c_zT(n):
            l = n // NG
            k, free = bank()
            for c in range(2):
                M["p10", n] = op("pe", lambda e, c=c: e.transpose(PS[:, k, c * 128:(c + 1) * 128],
                                                                  z[:, n % 2, c * 128:(c + 1) * 128], ident[:, :]),
                                 [M["z", n]] + free, "p10" if c else None)
            for c in range(2):
                m = op("act", lambda e, c=c: e.activation(
                    zf[:, n % 2, c, :], PS[:, k, c * 128:(c + 1) * 128], ACT.Identity, bias=V("lb", 2 * l + c),
                    scale=V("lg", 2 * l + c)), [M["p10", n], before("zT", n - 2)], "zf")
            held[k] = [m]
            used = before("p11", n // 2 - 1, 2)
            half = slice(n % 2 * 128, n % 2 * 128 + 128)
            h = high(zT[0][:, :, half], zf[:, n % 2, :, :], [m, used], "zTh")
            M["zT", n] = low(zT[1][:, :, half], zf[:, n % 2, :, :], zT[0][:, :, half], [h, used], "zTl", "pool")

        def c_mlp(m, part):
            l = 2 * m // NG
            kg, fg = bank()
            ka, fa = bank()
            if part < 2:
                j0 = 2 * part
                prods = [(kg, fg, i, 640 + (j0 + i) * 128, 128) for i in (0, 1)] + \
                        [(ka, fa, i, (j0 + i) * 128, 128) for i in (0, 1)]
                glus = [j0, j0 + 1]
            else:
                prods = [(kg, fg, 0, 640 + 512, 128), (kg, fg, 1, 1280, 106), (ka, fa, 0, 512, 128)]
                glus = [4, 5]
            for k, free, o, wcol, w in prods:
                for c in range(2):
                    done = mm3(PS[0:w, k, o * 256:o * 256 + 256],
                               lambda a, c=c, wcol=wcol, w=w: W1[a][:, c, wcol:wcol + w], lambda a, c=c: zT[a][:, c, :],
                               c == 0, c == 1, [M["zT", 2 * m], M["zT", 2 * m + 1], WREADY.get(("1", l))] + free,
                               "p11" if c else None)
                M["p11", m, part] = done
                if k == kg:
                    gdone = done
            for j in glus:
                lo, hi = (64, 64 + TAIL) if j == 5 else (0, 128)
                o = j % 2 * 256
                bi = vecs[lo:hi, VEC["b1g"] + 6 * l + j:VEC["b1g"] + 6 * l + j + 1]
                M["gl", m, j] = op("act", lambda e, lo=lo, hi=hi, o=o, bi=bi, j=j: e.activation(
                    Gl[lo:hi, j % 4, :], PS[lo:hi, kg, o:o + 256], ACT.Gelu, bias=bi),
                    [gdone] + ([M["u", m, 0]] if part == 2 else [before("u", m - 1, 2 - part), before("ut", m - 1)]), "gl")
            for j in glus:
                if j == 5:
                    s, w, gl = PS[0:TAIL, kg, 256:512], TAIL, Gl[64:64 + TAIL, 1, :]
                else:
                    s, w, gl = PS[:, ka, j % 2 * 256:j % 2 * 256 + 256], 128, Gl[:, j % 4, :]
                bi = vecs[0:w, VEC["b1a"] + 6 * l + j:VEC["b1a"] + 6 * l + j + 1]
                M["glu", m, part] = op("dve", lambda e, s=s, w=w, gl=gl, bi=bi, j=j: e.scalar_tensor_tensor(
                    out=Gl[0:w, j % 4, :], in0=s, scalar=bi, in1=gl, op0=ALU.add, op1=ALU.mult),
                    [M["p11", m, part], M["gl", m, j]], "glu")
            held[kg] = [M["glu", m, part], M["gl", m, glus[-1]]]
            held[ka] = [M["glu", m, part]]

        def c_u(m, part):
            used = before("p12", 2 * m - 1)
            A = slice(0, 128)
            parts = ((A, slice(2 * part, 2 * part + 2), slice(2 * part, 2 * part + 2)),) if part < 2 else \
                ((A, slice(4, 5), slice(0, 1)), (slice(0, TAIL), slice(5, 6), slice(1, 2)))
            for r, j, g in parts:
                h = high(uT[0][r, j, :], Gl[r, g, :], [M["glu", m, part], used], "uh")
                if r is A:
                    M["u", m, part] = low(uT[1][r, j, :], Gl[r, g, :], uT[0][r, j, :], [h, used], "ul", "pool")
                else:
                    M["ut", m] = low(uT[0][64:64 + TAIL, j, :], Gl[r, g, :], uT[0][r, j, :], [h, used], "ut")

        def c_w2(n):
            l, g, b, w = place(n)
            k, free = bank()
            cl = slice(n % 2 * 128, n % 2 * 128 + 128)
            ws = [M["u", n // 2, 0], M["u", n // 2, 1], M["u", n // 2, 2], M["ut", n // 2], WREADY.get(("2", l))] + free
            for j in range(5):
                mm3(PS[:, k, 0:256], lambda a, j=j: uT[a][:, j, cl], lambda a, j=j: W2[a][:, j, :], j == 0, False,
                    ws, None)
            op("pe", lambda e: e.matmul(PS[:, k, 0:256], uT[0][0:STK, 5, cl], W2[0][0:STK, 5, :], start=False,
                                        stop=False), ws)
            M["p12", n] = op("pe", lambda e: e.matmul(PS[:, k, 0:256], uT[0][0:TAIL + 1, 5, cl],
                                                      W2[1][0:TAIL + 1, 5, :], start=False, stop=True), ws, "p12")
            a = M["x3", n] = op("dve", lambda e: e.tensor_tensor(os_[:, n % 2, :], PS[:, k, 0:256], x2[:, n % NX, :],
                                                                 ALU.add),
                                [M["p12", n], before("sto", n - 2)], "x3")
            held[k] = [a]
            rows = slice(w * 128, (w + 1) * 128)
            if l == 0:
                M["sto", n] = M["sty", g] = dma(y_d[b, rows, :], os_[:, n % 2, :], [a], f"sto{n % 2}")
                return
            a = M["os", n] = op("pool", lambda e: e.tensor_tensor(os_[:, n % 2, :], os_[:, n % 2, :],
                                                                  x1i[:, n % 2, :], ALU.add),
                                [a, M["lx1", n]], "os")
            M["sto", n] = dma(out[b, rows, :], os_[:, n % 2, :], [a], f"sto{n % 2}")

        def reload(key, pairs, last):
            for dst, src in pairs:
                WREADY[key, 1] = dma(dst.bitcast(F32), src, [last, SPLIT_DONE[-1]], "w_re" + key)

        def at_switch(fn):
            return lambda n: fn(n) if n == NG - 1 else None

        re_q = at_switch(lambda n: reload("q", [(WQ[a][:, :, :], wq_d[a]) for a in (0, 1)], M["p2", n, 2]))
        re_o = at_switch(lambda n: reload("o", [(WO[a][:, :, :], wo_d[a]) for a in (0, 1)], M["p8", n]))
        re_1 = at_switch(lambda n: reload("1", [(W1[a][:, :, :], w1_d[a]) for a in (0, 1)], M["p11", n // 2, 2]))
        re_2 = at_switch(lambda n: reload("2", [(W2[a][r, j, :], w2_d[a][r, j, :]) for a in (0, 1) for r, j in (
            (slice(0, 128), slice(0, 5)), (slice(0, TAIL + 1 if a else STK), slice(5, 6)))], M["p12", n]))

        def pairs(stage, which):
            return lambda n, *rest: stage(n // 2 if which is None else n - 1 + which, *rest) if n % 2 else None

        def parity(stage, odd):
            return lambda n, *rest: stage(n, *rest) if n % 2 == odd else None

        ORDER = [
            (1, pre_y),
            (10, c_z), (9, c_stats), (3, a_scale),
            (8, c_wo), (8, re_o), (8, c_shift), (7, c_oT), (5, b_exp, 1), (11, parity(c_zT, 1)), (6, b_pv, 0),
            (12, pairs(c_mlp, None), 0), (13, pairs(c_w2, 0)),
            (5, b_turn, 0), (5, b_turn, 1), (12, pairs(c_u, None), 0), (6, b_pv, 1),
            (12, pairs(c_mlp, None), 1), (13, pairs(c_w2, 1)), (13, re_2),
            (5, b_turn, 2), (5, b_turn, 3), (12, pairs(c_u, None), 1), (12, pairs(c_mlp, None), 2), (12, re_1),
            (4, b_scores, 0), (2, a_qkv, 1), (2, a_square, 1), (4, b_scores, 1), (12, pairs(c_u, None), 2), (0, pre_norm),
            (3, a_qkT, 1), (2, a_rope, 1), (3, a_qkT_parts, 1), (2, a_qkv, 0), (2, a_square, 0), (3, a_qkT, 0), (3, a_qkT_parts, 0),
            (3, a_stack, 1), (3, a_stack, 0), (2, a_rope, 0),
            (2, a_qkv, 2), (2, re_q), (2, a_v), (4, b_exp, 0), (2, a_sums), (2, a_rot),
            (1, a_rt), (1, a_hT), (11, parity(c_zT, 0)), (0, pre_mm),
            (12, load_x1), (0, load_tab), (0, load_y)]
        loads(0)
        load_x(0)
        for t in range(U + 14):
            if t + 1 < U:
                loads(t + 1)
                load_x(t + 1)
            for d, stage, *rest in ORDER:
                if 0 <= t - d < U:
                    stage(t - d, *rest)
        op("sp", None, [M["sto", U - 1], M["sto", U - 2], M["stx", NG - 1], M["stx", NG - 2]])

        block = ctx.enter_context(nc.Block())

        @block.sync
        def _(e):
            Q.run("sp", e)

        @block.tensor
        def _(e):
            Q.run("pe", e)

        @block.scalar
        def _(e):
            Q.run("act", e)

        @block.vector
        def _(e):
            Q.run("dve", e)

        @block.gpsimd
        def _(e):
            Q.run("pool", e)


def constants():
    f = np.float32
    half = np.arange(0, 64, 2, dtype=f)
    inv = (f(1.0) / np.power(f(10000.0), half / f(64))).astype(f)
    t = np.arange(T, dtype=f)
    fr = t[:, None] * inv[None, :]
    fr = np.concatenate([fr, fr], -1).astype(np.float64)
    base = ((half + f(0.4 * 64)) / f(1.4 * 64)).astype(f)
    power = ((t - f(T // 2)) / f(64.0)).astype(f)
    scale = base.astype(np.float64)[None, :] ** power.astype(np.float64)[:, None]
    scale = np.concatenate([scale, scale], -1)
    sgn = np.concatenate([-np.ones(32), np.ones(32)])[None, :]
    cos, sin = np.cos(fr), np.sin(fr) * sgn
    tab = np.concatenate([cos * scale, sin * scale, cos / scale, sin / scale], -1).astype(f)
    ident = np.eye(128, dtype=f)
    grp = np.kron(np.eye(8), np.full((16, 16), 1.0 / 16)).astype(f)
    i, j = np.arange(128)[:, None], np.arange(128)[None, :]
    cur = np.where(i >= j, 0.0, MASKED)
    prv = np.where(i <= j, 0.0, MASKED)
    mask = np.zeros((128, 2, 256), f)
    mask[:, 0, 0:128], mask[:, 0, 128:256] = cur, prv
    mask[:, 1, 128:256], mask[:, 1, 0:128] = cur, prv
    return tab, ident, grp, mask


def kernel(**inputs):
    import numpy as _np
    import concourse.bacc as _bacc
    from concourse import mybir as _mybir
    from concourse.bass_utils import run_bass_kernel_spmd as _run

    a = {k: _np.asarray(v) for k, v in inputs.items()}

    def per_partition(v):
        return v.reshape(-1, 128).T

    vec = _np.zeros((128, NVEC), _np.float32)
    for name, key in (("mix_r", "L0_attn_time_mix_r"), ("mix_k", "L0_attn_time_mix_k"),
                      ("mix_v", "L0_attn_time_mix_v"), ("decay", "L0_attn_time_decay"),
                      ("first", "L0_attn_time_first"), ("gamma", "L0_attn_ln_gamma"), ("beta", "L0_attn_ln_beta")):
        vec[:, VEC[name]:VEC[name] + 2] = per_partition(a[key].reshape(-1))
    vec[:, VEC["lg"]:VEC["lg"] + 4] = per_partition(a["L0_ffn_ln_g"].reshape(-1))
    vec[:, VEC["lb"]:VEC["lb"] + 4] = per_partition(a["L0_ffn_ln_b"].reshape(-1))
    for l in range(2):
        b1 = a["L0_ffn_b1"][l]
        for name, o, row in (("b1a", 0, 0), ("b1g", HID, 64)):
            c = VEC[name] + 6 * l
            vec[:, c:c + 5] = per_partition(b1[o:o + 640])
            vec[row:row + TAIL, c + 5] = b1[o + 640:o + HID]
    qs, ks = a["L0_ffn_q_scale"], a["L0_ffn_k_scale"]
    row = _np.concatenate([qs, _np.roll(qs, 32, 1), ks, _np.roll(ks, 32, 1)], 1)
    qsk = _np.ascontiguousarray(_np.broadcast_to(row[None], (128, 2, 256)))
    wrkvo = _np.stack([a["L0_attn_W_" + n].T for n in "rkvo"])
    tab, ident, grp, mask = constants()
    arrays = {"x": a["L0_attn_x"], "wrkvo": wrkvo, "wqkv": a["L0_ffn_wqkv"], "wo": a["L0_ffn_wo"],
              "w1": a["L0_ffn_w1"], "w2": a["L0_ffn_w2"], "b2": a["L0_ffn_b2"], "vec": vec, "qsk": qsk, "tab": tab,
              "ident_d": ident, "grp_d": grp, "mask_d": mask}
    arrays = {k: _np.ascontiguousarray(v) for k, v in arrays.items()}
    nc = _bacc.Bacc("TRN2", target_bir_lowering=False, num_devices=1)
    args = {k: nc.dram_tensor(k, v.shape, _mybir.dt.from_np(v.dtype), kind="ExternalInput").ap()
            for k, v in arrays.items()}
    o = nc.dram_tensor("out_dram", (NB, T, C), _mybir.dt.float32, kind="ExternalOutput").ap()
    build(nc, out=o, **args)
    r = _run(nc, [arrays], core_ids=[0])
    return r.results[0]["out_dram"]
```
